# Optimizing a Trainium2 kernel written in Bass

```python
import numpy as np
import jax
import jax.numpy as jnp

def _softmax(x, axis=-1):
    return jax.nn.softmax(x, axis=axis)

def _gelu(x):
    return jax.nn.gelu(x, approximate=True)

def _silu(x):
    return jax.nn.silu(x)

def _sigmoid(x):
    return jax.nn.sigmoid(x)

def _layernorm(x, axis=-1, eps=1e-05):
    m = jnp.mean(x, axis=axis, keepdims=True)
    v = jnp.var(x, axis=axis, keepdims=True)
    return (x - m) / jnp.sqrt(v + eps)

def _scatter_add(tgt, idx, src, axis=0):
    return tgt.at[idx].add(src)

def _segment_sum(src, seg, n):
    return jax.ops.segment_sum(src, seg, n)
kernel_name = 'mk_adj_preln_d2_adj_r2_6e9f27'

def setup_inputs(seed: int=0):
    np.random.seed(seed)
    _w = jnp.asarray

    def _rec_inputs():
        import jax
        import jax.numpy as jnp
        _gk = jax.random.key(seed)
        x = -0.0002928 + 1 * jax.random.normal(jax.random.fold_in(_gk, 1), (16, 512, 256), jnp.float32)
        _w = (1.0 + jnp.arange(512, dtype=jnp.float32)) ** (-0.5)
        _w = _w / _w.mean()
        _pij = jnp.clip(0.00390625 * _w[:, None] * _w[None, :], 0.0, 1.0)
        _a = jax.random.uniform(jax.random.fold_in(_gk, 2), (16, 512, 512)) < _pij
        adj = _a
        return (x, adj)
    x, adj = _rec_inputs()

    def _L0_gnn_setup():
        import jax, jax.numpy as jnp
        import numpy as np
        QUERY_DIM = 256
        HEADS = 4
        DIM_HEAD = 64
        INNER = HEADS * DIM_HEAD
        B, N = (4, 1024)
        key = jax.random.key(seed)
        ks = jax.random.split(key, 6)
        s = 1.0 / np.sqrt(QUERY_DIM)
        x = jax.random.normal(ks[0], (B, N, QUERY_DIM), dtype=jnp.float32)
        adjacency_mask = jax.random.randint(ks[1], (B, N, N), 0, 2) > 0
        Wq = jax.random.normal(ks[2], (QUERY_DIM, INNER), dtype=jnp.float32) * s
        Wk = jax.random.normal(ks[3], (QUERY_DIM, INNER), dtype=jnp.float32) * s
        Wv = jax.random.normal(ks[4], (QUERY_DIM, INNER), dtype=jnp.float32) * s
        Wo = jax.random.normal(ks[5], (INNER, QUERY_DIM), dtype=jnp.float32) * (1.0 / np.sqrt(INNER))
        bo = jnp.zeros((QUERY_DIM,), dtype=jnp.float32)
        return {'x': x, 'adjacency_mask': adjacency_mask, 'Wq': Wq, 'Wk': Wk, 'Wv': Wv, 'Wo': Wo, 'bo': bo}
    _L0_gnn_all = _L0_gnn_setup()
    _L0_gnn_in = {k: v for k, v in _L0_gnn_all.items() if k in ('Wq', 'Wk', 'Wv', 'Wo', 'bo')}
    del _L0_gnn_all

    def _L1_gnn_setup():
        import jax, jax.numpy as jnp
        import numpy as np
        HEAD_NUM = 8
        THRESHOLD = 0.1
        NEG = -10000000000.0
        COS_EPS = 1e-08
        B, S, D = (8, 512, 256)
        D_OUT = 256
        key = jax.random.key(seed)
        ks = jax.random.split(key, 12)
        embs = jax.random.normal(ks[0], (B, S, D), dtype=jnp.float32)
        lengths = jax.random.randint(ks[1], (B,), S // 2, S + 1)
        pad = jnp.arange(S)[None, :] >= lengths[:, None]
        score_mask = pad[:, :, None] | pad[:, None, :]
        sc = 1.0 / np.sqrt(D)
        mk = lambda k, shp: jax.random.normal(k, shp, dtype=jnp.float32) * sc
        return {'embs': embs, 'score_mask': score_mask, 'map_w': mk(ks[2], (D, D)), 'map_b': jnp.zeros((D,), jnp.float32), 'q_w': mk(ks[3], (D, D)), 'q_b': jnp.zeros((D,), jnp.float32), 'k_w': mk(ks[4], (D, D)), 'k_b': jnp.zeros((D,), jnp.float32), 'gcn_map_w': mk(ks[5], (D_OUT, D)), 'gcn_map_b': jnp.zeros((D_OUT,), jnp.float32), 'gcn_W': jax.random.normal(ks[6], (D_OUT // HEAD_NUM, D_OUT // HEAD_NUM), dtype=jnp.float32) * (1.0 / np.sqrt(D_OUT // HEAD_NUM))}
    _L1_gnn_all = _L1_gnn_setup()
    _L1_gnn_in = {k: v for k, v in _L1_gnn_all.items() if k in ('map_w', 'map_b', 'q_w', 'q_b', 'k_w', 'k_b', 'gcn_map_w', 'gcn_map_b', 'gcn_W')}
    del _L1_gnn_all
    return {'x': x, 'adj': adj, 'L0_gnn_Wq': _L0_gnn_in['Wq'], 'L0_gnn_Wk': _L0_gnn_in['Wk'], 'L0_gnn_Wv': _L0_gnn_in['Wv'], 'L0_gnn_Wo': _L0_gnn_in['Wo'], 'L0_gnn_bo': _L0_gnn_in['bo'], 'L1_gnn_map_w': _L1_gnn_in['map_w'], 'L1_gnn_map_b': _L1_gnn_in['map_b'], 'L1_gnn_q_w': _L1_gnn_in['q_w'], 'L1_gnn_q_b': _L1_gnn_in['q_b'], 'L1_gnn_k_w': _L1_gnn_in['k_w'], 'L1_gnn_k_b': _L1_gnn_in['k_b'], 'L1_gnn_gcn_map_w': _L1_gnn_in['gcn_map_w'], 'L1_gnn_gcn_map_b': _L1_gnn_in['gcn_map_b'], 'L1_gnn_gcn_W': _L1_gnn_in['gcn_W']}

def reference(x, adj, L0_gnn_Wq, L0_gnn_Wk, L0_gnn_Wv, L0_gnn_Wo, L0_gnn_bo, L1_gnn_map_w, L1_gnn_map_b, L1_gnn_q_w, L1_gnn_q_b, L1_gnn_k_w, L1_gnn_k_b, L1_gnn_gcn_map_w, L1_gnn_gcn_map_b, L1_gnn_gcn_W):
    import jax
    import jax.numpy as jnp

    def _L0_gnn_ref(x, adjacency_mask, Wq, Wk, Wv, Wo, bo):
        import jax, jax.numpy as jnp
        import numpy as np
        QUERY_DIM = 256
        HEADS = 4
        DIM_HEAD = 64
        INNER = HEADS * DIM_HEAD
        B, N = (4, 1024)
        scale = DIM_HEAD ** (-0.5)

        def split_heads(t):
            b, n, _ = t.shape
            return t.reshape(b, n, HEADS, DIM_HEAD).transpose(0, 2, 1, 3)
        q = split_heads(x @ Wq)
        k = split_heads(x @ Wk)
        v = split_heads(x @ Wv)
        sim = jnp.einsum('bhid,bhjd->bhij', q, k) * scale
        neg = -jnp.finfo(sim.dtype).max
        sim = jnp.where(adjacency_mask[:, None, :, :], sim, neg)
        attn = jax.nn.softmax(sim, axis=-1)
        out = jnp.einsum('bhij,bhjd->bhid', attn, v)
        out = out.transpose(0, 2, 1, 3).reshape(x.shape[0], x.shape[1], INNER)
        return out @ Wo + bo

    def _L1_gnn_ref(embs, score_mask, map_w, map_b, q_w, q_b, k_w, k_b, gcn_map_w, gcn_map_b, gcn_W):
        import jax, jax.numpy as jnp
        import numpy as np
        HEAD_NUM = 8
        THRESHOLD = 0.1
        NEG = -10000000000.0
        COS_EPS = 1e-08
        B, S, D = (8, 512, 256)
        D_OUT = 256
        b, s, d = embs.shape
        h, dk = (HEAD_NUM, d // HEAD_NUM)
        sm = score_mask[:, None, :, :]
        keep = (~sm[..., 0:1]).astype(embs.dtype)
        m = embs @ map_w.T + map_b
        sem = m.reshape(b, s, h, dk).transpose(0, 2, 1, 3)
        norm = jnp.maximum(jnp.linalg.norm(sem, axis=-1, keepdims=True), COS_EPS)
        n = sem / norm
        cos = jnp.einsum('bhsd,bhtd->bhst', n, n)
        cos = cos * (~sm).astype(cos.dtype)
        cos_adj = (cos > THRESHOLD).astype(embs.dtype)
        q = (m @ q_w.T + q_b).reshape(b, s, h, dk).transpose(0, 2, 1, 3)
        k = (m @ k_w.T + k_b).reshape(b, s, h, dk).transpose(0, 2, 1, 3)
        scores = jnp.einsum('bhsd,bhtd->bhst', q, k) / jnp.sqrt(jnp.asarray(dk, embs.dtype))
        scores = jnp.where(sm, NEG, scores)
        p_attn = jax.nn.softmax(scores, axis=-1) * keep
        adj = cos_adj * p_attn
        hk = gcn_map_w.shape[0] // h
        sem_h = (embs @ gcn_map_w.T + gcn_map_b).reshape(b, s, h, hk).transpose(2, 0, 1, 3)
        adj_h = adj.transpose(1, 0, 2, 3)
        Ax = jnp.einsum('hbst,hbtd->hbsd', adj_h, sem_h)
        AxW = Ax @ gcn_W.T
        denom = adj_h.sum(-1, keepdims=True) + 1.0
        out = jax.nn.relu(AxW / denom)
        out = out.transpose(1, 2, 0, 3).reshape(b, s, h * hk)
        return out
    h = jnp.maximum(_layernorm(x, axis=-1), 0.0)
    x = x + _L0_gnn_ref(h, adj, L0_gnn_Wq, L0_gnn_Wk, L0_gnn_Wv, L0_gnn_Wo, L0_gnn_bo)
    h = jnp.maximum(_layernorm(x, axis=-1), 0.0)
    x = x + _L1_gnn_ref(h, adj, L1_gnn_map_w, L1_gnn_map_b, L1_gnn_q_w, L1_gnn_q_b, L1_gnn_k_w, L1_gnn_k_b, L1_gnn_gcn_map_w, L1_gnn_gcn_map_b, L1_gnn_gcn_W)
    return x

_drawn_inputs = setup_inputs


def setup_inputs(seed=0):
    import zlib

    import numpy as np

    out = dict(_drawn_inputs(seed))
    spreads = {'L0_gnn_bo': (0.0, 0.1),
     'L1_gnn_map_b': (0.0, 0.8),
     'L1_gnn_q_b': (0.0, 0.8),
     'L1_gnn_k_b': (0.0, 0.8),
     'L1_gnn_gcn_map_b': (0.0, 0.294)}
    factors = {'L1_gnn_map_w': 7.55, 'L1_gnn_q_w': 8.0, 'L1_gnn_k_w': 8.0}
    for name, (base, spread) in spreads.items():
        noise = np.random.default_rng([zlib.crc32(name.encode()), seed]).standard_normal(out[name].shape)
        drawn = base * np.exp(spread * noise) if base else spread * noise
        out[name] = jnp.asarray(drawn.astype(out[name].dtype))
    for name, factor in factors.items():
        out[name] = (out[name] * factor).astype(out[name].dtype)
    return out
```

```python
from contextlib import ExitStack

import concourse.bass as bass
from concourse import mybir

F32 = mybir.dt.float32
F32R = mybir.dt.float32r
BF16 = mybir.dt.bfloat16
U8 = mybir.dt.uint8
ALU = mybir.AluOpType
ACT = mybir.ActivationFunctionType
AX_X = mybir.AxisListType.X

P = 128
BANK = 512
NEG0 = -3.3895e38
NEG1 = -1e10
LN_EPS = 1e-5
NORM_FLOOR = 1e-16
COS_MIN = 0.1
BIG = 3.4e38

Y_SLOTS, X_SLOTS = 32, 16
N_SLOTS = Y_SLOTS + X_SLOTS
GROUP = 8
LAG_SELECT, LAG_TURN, LAG_PV = 1, 2, 3

SLOTS = {
    0: [("h0_turn", 1, 0)], 1: [("add_bo", 0, 0), ("h0_turn", 1, 1)],
    3: [("v0", 1, 0)], 4: [("v0", 1, 1)],
    5: [("out_proj", 0, 0)], 6: [("out_proj", 0, 1)], 7: [("ln1_stats", 0, 0)],
    8: [("ln1_apply", 0, 0), ("q0", 1, 0)], 9: [("q0", 1, 1)],
    11: [("k0", 1, 0)], 12: [("mask0", 1, 0), ("k0", 1, 1)],
    13: [("h1_turn", 0, 0)], 14: [("h1_turn", 0, 1)],
    15: [("m", 0, 0)], 16: [("m", 0, 1)],
    17: [("m_square", 0, 0)], 18: [("m_sums", 0, 0), ("m_norms", 0, 0)],
    19: [("m_turn", 0, 0)], 20: [("m_turn", 0, 1)],
    22: [("q1", 0, 0)], 23: [("q1", 0, 1)],
    24: [("n_scale", 0, 0), ("k1", 0, 0)], 25: [("k1", 0, 1)],
    28: [("n_turn", 0, 0)], 29: [("n_turn", 0, 1)],
    33: [("row_factors", -1, 0)],
    34: [("mask1", 0, 0), ("ln0_stats", 2, 0)], 35: [("ln0_apply", 2, 0)],
    36: [("finish", -1, 0)], 37: [("finish", -1, 1)],
    38: [("keep_x1", 0, 0), ("v1", 0, 0)], 39: [("v1", 0, 1)],
}
FIRST_SLOT = [("ln0_stats", 1, 0), ("ln0_apply", 1, 0), ("fold", 0, 0), ("fold", 0, 1)]
PSUM_TASKS = {"h0_turn": "act", "v0": "act", "out_proj": "dve", "q0": "dve", "k0": "dve",
              "h1_turn": "act", "m": "dve", "m_turn": "act", "q1": "dve", "k1": "dve",
              "n_turn": "dve", "finish": "dve", "v1": "dve", "fold": "dve", "pv": "act"}


class Body:

    def __init__(self, k, graphs, before):
        self.units = [None] * N_SLOTS
        if k >= 1:
            self.units[:Y_SLOTS] = [("Y", u) for u in range(Y_SLOTS)]
        if k + 1 < graphs:
            self.units[Y_SLOTS:] = [("X", u) for u in range(X_SLOTS)]
        self.before = before
        self.tasks = []
        self.last = 0
        for s in range(N_SLOTS):
            here = list(FIRST_SLOT) if k == -1 and s == 0 else []
            for task, ahead, part in SLOTS.get(s, []):
                if 0 <= k + ahead < graphs:
                    here.append((task, ahead, part))
            done = self.lagged(s, LAG_PV)
            if done and done[1] % GROUP == GROUP - 1:
                here.append(("pv", done[0], done[1] // GROUP))
            self.tasks.append(here)
        self.bank_tasks = [(s, t) for s, here in enumerate(self.tasks) for t in here if t[0] in PSUM_TASKS]
        self.n_units = sum(u is not None for u in self.units)

    def lagged(self, s, lag):
        if s >= lag:
            return self.units[s - lag]
        return self.before.units[N_SLOTS + s - lag] if self.before else None

    def unit_number(self, s):
        return sum(u is not None for u in self.units[:s])

    def lagged_number(self, s, lag):
        if s >= lag:
            return self.unit_number(s - lag)
        return self.before.unit_number(N_SLOTS + s - lag) - self.before.n_units

    def emptied(self, engine):
        return sum(PSUM_TASKS[t[0]] == engine for _, t in self.bank_tasks)


class At:

    def __init__(self, k, body, units, banks, emptied, first=None, step=None):
        self.k, self.body = k, body
        self.first = k if first is None else first
        self.n_units, self.n_banks, self.n_emptied, self.step = units, banks, emptied, step

    def _passes(self, value, per_pass):
        return value if self.step is None else (self.k - self.first) * per_pass + value

    def units(self, n):
        return self._passes(self.n_units + n, self.step and self.step[0])

    def unit_ring(self, n, size):
        return (self.n_units + n) % size

    def banks(self, n):
        return self._passes(self.n_banks + n, self.step and self.step[1])

    def bank_ring(self, n):
        return (self.n_banks + n) % 2

    def _emptied(self, engine, n):
        return self._passes(self.n_emptied[engine] + n, self.step and self.step[2][engine])

    def emptied(self, i):
        tasks = self.body.bank_tasks if i >= 0 else self.body.before.bank_tasks
        engine = PSUM_TASKS[tasks[i][1][0]]
        if i >= 0:
            return engine, self._emptied(engine, sum(PSUM_TASKS[t[0]] == engine for _, t in tasks[:i + 1]))
        return engine, self._emptied(engine, 1 - sum(PSUM_TASKS[t[0]] == engine for _, t in tasks[i:]))

    def latest(self, s, task, part=None, which=None):
        def found(tasks, until):
            return [i for i, (at, t) in enumerate(tasks)
                    if at <= until and t[0] == task and part in (None, t[2]) and which in (None, t[1])]
        here = found(self.body.bank_tasks, s)
        if here:
            return here[-1]
        before = self.body.before.bank_tasks
        return found(before, N_SLOTS)[-1] - len(before)

    def graph(self, ahead, each, plus):
        return (self.k + ahead) * each + plus


def attention_layers(nc, x, adj, wq, wk, wv, wo, bo, map_w, map_b, q_w, q_b, k_w, k_b,
                     gcn_w, gcn_b, gcn_head_w, out):
    graphs, tokens, dim = x.shape
    QT = tokens // P
    DC = dim // P
    H0, H1 = 4, 8
    D0, D1 = dim // H0, dim // H1
    HC0, HC1 = H0 // DC, H1 // DC
    HALF = tokens // 2
    C0, C1 = float(D0) ** -0.5, float(D1) ** -0.5
    DMA = 16
    WEIGHT_DMAS = 13 * DMA
    Q0_DMAS, K0_DMAS = 2 * HC0 * DMA, 4 * HC0 * DMA
    STACK_DMAS = 4 * HC1 * DMA
    assert (QT, DC, D0, D1, tokens) == (4, 2, 64, 32, BANK)

    body_first = Body(-1, graphs, None)
    body_0 = Body(0, graphs, body_first)
    body_loop = Body(1, graphs, body_0)
    body_14 = Body(graphs - 2, graphs, body_loop)
    body_15 = Body(graphs - 1, graphs, body_14)
    body_16 = Body(graphs, graphs, body_15)
    LOOP_FROM, LOOP_TO = 1, graphs - 2
    ats, units, banks, emptied = {}, 0, 0, {"act": 0, "dve": 0}
    for name, k, body, passes in (("first", -1, body_first, 1), ("0", 0, body_0, 1),
                                  ("loop", 1, body_loop, LOOP_TO - LOOP_FROM),
                                  ("14", graphs - 2, body_14, 1), ("15", graphs - 1, body_15, 1),
                                  ("16", graphs, body_16, 1)):
        ats[name] = (k, body, units, banks, dict(emptied))
        units += passes * body.n_units
        banks += passes * len(body.bank_tasks)
        for e in emptied:
            emptied[e] += passes * body.emptied(e)
    loop_step = (body_loop.n_units, len(body_loop.bank_tasks), {e: body_loop.emptied(e) for e in emptied})
    assert loop_step[0] % 4 == 0 and loop_step[1] % 2 == 0
    tail = [[t for s, t in b.bank_tasks if s >= Y_SLOTS + 6] for b in (body_0, body_loop)]
    assert tail[0] == tail[1], tail

    def walk(engine, emit):
        for name in ("first", "0"):
            emit(At(*ats[name]))
        with engine.Fori(LOOP_FROM, LOOP_TO) as k:
            emit(At(k, *ats["loop"][1:], first=LOOP_FROM, step=loop_step))
        for name in ("14", "15", "16"):
            emit(At(*ats[name]))

    ctx = ExitStack()
    with ctx:
        def sb(name, shape, dt=F32):
            return ctx.enter_context(nc.sbuf_tensor(name, shape, dt))

        def sem(name):
            return ctx.enter_context(nc.semaphore(name))

        wq_sb, wk_sb, wv_sb, wo_sb = (sb(n, [P, DC, dim]) for n in ("wq_sb", "wk_sb", "wv_sb", "wo_sb"))
        map_sb, qw_sb, kw_sb = (sb(n, [P, DC, dim]) for n in ("map_sb", "qw_sb", "kw_sb"))
        gcn_sb = sb("gcn_sb", [P, DC, dim])
        head_blocks = sb("head_blocks", [P, P])
        gcn_b_col = sb("gcn_b_col", [P, DC])
        gcn_b_wide = sb("gcn_b_wide", [P, DC, P])
        bo_row, map_b_row, gcn_b_row = (sb(n, [P, dim]) for n in ("bo_row", "map_b_row", "gcn_b_row"))
        q_b_col, k_b_col = sb("q_b_col", [P, DC]), sb("k_b_col", [P, DC])
        ident = sb("ident", [P, P])
        minus_half = sb("minus_half", [P, QT * H1])
        q0_stack, k0_high, k0_low = (sb(n, [P, H0, tokens], F32R) for n in ("q0_stack", "k0_high", "k0_low"))
        q1_stack, k1_stack, ns_stack, nm_stack = (
            sb(n, [P, H1, tokens], F32R) for n in ("q1_stack", "k1_stack", "ns_stack", "nm_stack"))
        q_parts, k_parts, n_parts = (sb(n, [P, 2, DC, tokens]) for n in ("q_parts", "k_parts", "n_parts"))
        h_t = sb("h_t", [P, DC, tokens])
        tok = sb("tok", [P, QT, dim])
        m_t = sb("m_t", [P, DC, tokens])
        v0, v1 = sb("v0_sb", [P, QT, dim]), sb("v1_sb", [P, QT, dim])
        x_now = sb("x_now", [P, QT, dim])
        x1_kept = sb("x1_kept", [P, QT, dim])
        o_t = sb("o_t", [P, DC, tokens])
        y = sb("y", [P, QT, dim])
        adj_raw = sb("adj_raw", [P, QT, tokens], U8)
        mask0, mask1 = sb("mask0_sb", [P, QT, tokens], BF16), sb("mask1_sb", [P, QT, tokens], BF16)
        prob = sb("prob", [P, 4, tokens])
        prob_t = sb("prob_t", [P, 2 * QT * tokens])
        prob_t_x = prob_t[:, :].rearrange("p (h c q) -> p h c q", h=2, c=QT)
        prob_t_y = prob_t[:, :].rearrange("p (h c q) -> p h c q", h=4, c=QT)
        gcn_raw = prob_t[:, 0:DC * dim].rearrange("p (c n) -> p c n", c=DC)
        row_min = sb("row_min", [P, 4])
        sum0, inv0 = sb("sum0", [P, X_SLOTS]), sb("inv0", [P, X_SLOTS])
        sum1, picked1 = sb("sum1", [P, QT, H1]), sb("picked1", [P, QT, H1])
        factor, keep_row = sb("factor", [P, QT, H1]), sb("keep_row", [P, QT])
        stats = sb("stats", [P, QT, 6])
        mean_var = [sb("mean_var0", [P, QT, 2]), sb("mean_var1", [P, QT, 2])]
        minus_mean, var_eps, rstd = sb("minus_mean", [P, QT]), sb("var_eps", [P, QT]), sb("rstd", [P, QT])
        norm2, floored, inv_norm = (sb(n, [P, QT * H1]) for n in ("norm2", "floored", "inv_norm"))

        def bank(name):
            return ctx.enter_context(nc.psum_tensor(name, [P, BANK], F32))

        score_bank = [bank("score0"), bank("score1")]
        cos_bank = [bank("cos0"), bank("cos1")]
        turn_bank = [bank("turn0"), bank("turn1")]
        work_bank = [bank("work0"), bank("work1")]

        weights_loaded, blocks_zeroed, blocks_loaded = sem("weights_loaded"), sem("blocks_zeroed"), sem("blocks_loaded")
        ident_zeroed, consts_made, bias_widened = sem("ident_zeroed"), sem("consts_made"), sem("bias_widened")
        waits_passed = sem("waits_passed")
        scores_ready, masked, exped, turned, turn_copied = (
            sem(n) for n in ("scores_ready", "masked", "exped", "turned", "turn_copied"))
        inverted, normed = sem("inverted"), sem("normed")
        cos_ready, picked = sem("cos_ready"), sem("picked")
        bank_filled = sem("bank_filled")
        bank_emptied = {"act": sem("bank_emptied_act"), "dve": sem("bank_emptied_dve")}
        tok_loaded, x_loaded, adj_loaded, y_stored = (
            sem(n) for n in ("tok_loaded", "x_loaded", "adj_loaded", "y_stored"))
        stats_taken = [sem("stats0_taken"), sem("stats1_taken")]
        stats_ready = [sem("stats0_ready"), sem("stats1_ready")]
        norm_step = [sem("norm0_step"), sem("norm1_step")]
        normalised = [sem("normalised0"), sem("normalised1")]
        high_ready = {n: sem(n + "_high_ready") for n in ("q0", "k0", "q1", "k1", "n_turn")}
        q0_stacked, k0_stacked = sem("q0_stacked"), sem("k0_stacked")
        stacked = [sem(f"stacked{j}") for j in range(HC1)]
        bo_added, x1_copied = sem("bo_added"), sem("x1_copied")
        masks_made = sem("masks_made")
        squared, summed, norms_floored, inv_norm_ready, n_ready = (
            sem(n) for n in ("squared", "summed", "norms_floored", "inv_norm_ready", "n_ready"))
        factor_step, factors_ready, y_ready = sem("factor_step"), sem("factors_ready"), sem("y_ready")

        def unit_x(u):
            pair, rest = divmod(u, GROUP)
            return pair * 2 + rest % 2, rest % 2, rest // 2

        def unit_y(u):
            group, rest = divmod(u, GROUP)
            j, q2 = divmod(rest, 2)
            return (group // 2) * HC1 + j, j, (group % 2) * 2 + q2, q2

        def graph_ahead(s, lag, kind):
            return {"X": 1, "Y": -1}[kind] - (1 if s < lag else 0)

        def mask_number(at, layer):
            if at.first < 0:
                return 1
            return at.graph(0, 2, 2 + (layer if at.first + 1 < graphs else 0))

        def wait_out(eng, at, i):
            engine, count = at.emptied(i)
            eng.wait_ge(bank_emptied[engine], count)

        def wait_apart(eng):
            eng.sem_inc(waits_passed, 1)

        block = ctx.enter_context(nc.Block())

        @block.sync
        def _(sp):
            x_tiles = x.rearrange("b (t p) d -> b p t d", p=P)
            out_tiles = out.rearrange("b (t p) d -> b p t d", p=P)
            adj_tiles = adj.rearrange("b (t p) k -> b p t k", p=P)

            def of(tiles, g):
                return tiles[bass.ds(g, 1)].rearrange("a p t d -> (a p) t d")

            def stack_layer0(at):
                def rows(dst, parts, g, which, j, done):
                    sp.dma_start(dst[D0 * g:D0 * g + D0, j:H0:HC0, :].bitcast(F32),
                                 parts[D0 * j:D0 * j + D0, which, :, :]).then_inc(done, DMA)

                wait_out(sp, at, at.latest(N_SLOTS, "q0", 1))
                wait_apart(sp)
                if at.first >= 0:
                    sp.wait_ge(normed, at.graph(1, X_SLOTS, 0))
                for j in range(HC0):
                    for g in range(2):
                        rows(q0_stack, q_parts, g, g, j, q0_stacked)
                wait_out(sp, at, at.latest(N_SLOTS, "k0", 1))
                for j in range(HC0):
                    for g in range(2):
                        rows(k0_high, k_parts, g, 0, j, k0_stacked)
                        rows(k0_low, k_parts, g, 1, j, k0_stacked)

            def stack_layer1(at, j):
                if at.first >= 1:
                    sp.wait_ge(cos_ready, at.graph(-1, Y_SLOTS, 3 * GROUP + 2 * j + 2))
                stationary, moving = (0, 0, 1, 1), (0, 1, 0, 1)
                for dst, parts, rows in ((q1_stack, q_parts, stationary), (k1_stack, k_parts, moving),
                                         (ns_stack, n_parts, stationary), (nm_stack, n_parts, moving)):
                    for g, which in enumerate(rows):
                        sp.dma_start(dst[D1 * g:D1 * g + D1, j:H1:HC1, :].bitcast(F32),
                                     parts[D1 * j:D1 * j + D1, which, :, :]).then_inc(stacked[j], DMA)

            def load_adj(at, ahead, layer):
                if at.first >= 0:
                    sp.wait_ge(masks_made, mask_number(at, layer) - 1)
                wait_apart(sp)
                sp.dma_start(adj_raw[:, :, :], of(adj_tiles, at.k + ahead)).then_inc(adj_loaded, DMA)

            sp.dma_start(tok[:, :, :], of(x_tiles, 0)).then_inc(tok_loaded, DMA)
            for dst, src in ((wq_sb[:, :, :], wq), (wk_sb[:, :, :], wk), (wv_sb[:, :, :], wv), (gcn_raw, gcn_w),
                             (wo_sb[:, :, :], wo), (map_sb[:, :, :], map_w), (qw_sb[:, :, :], q_w),
                             (kw_sb[:, :, :], k_w)):
                sp.dma_start(dst, src.rearrange("(c p) n -> p c n", p=P)).then_inc(weights_loaded, DMA)
            for dst, src in ((q_b_col, q_b), (k_b_col, k_b), (gcn_b_col, gcn_b)):
                sp.dma_start(dst[:, :], src).then_inc(weights_loaded, DMA)
            for dst, src in ((bo_row, bo), (map_b_row, map_b)):
                sp.dma_start(dst[:, :], src.partition_broadcast(P)).then_inc(weights_loaded, DMA)
            sp.wait_ge(blocks_zeroed, 1)
            for g in range(HC1):
                sp.dma_start(head_blocks[D1 * g:D1 * g + D1, D1 * g:D1 * g + D1], gcn_head_w).then_inc(blocks_loaded, DMA)
            sp.dma_start(x_now[:, :, :], of(x_tiles, 0)).then_inc(x_loaded, DMA)

            def emit(at):
                first, k = at.first, at.k
                has_next, has_this = first + 1 < graphs, 0 <= first < graphs
                if has_next:
                    load_adj(at, 1, 0)
                    stack_layer0(at)
                if has_this:
                    load_adj(at, 0, 1)
                if first + 2 < graphs:
                    wait_out(sp, at, at.latest(N_SLOTS, "h0_turn" if first < 0 else "n_turn", 1))
                    wait_apart(sp)
                    sp.dma_start(tok[:, :, :], of(x_tiles, k + 2)).then_inc(tok_loaded, DMA)
                if has_this:
                    wait_out(sp, at, at.latest(N_SLOTS, "n_turn", 1))
                    stack_layer1(at, 0)
                    stack_layer1(at, 1)
                    if has_next:
                        sp.wait_ge(x1_copied, at.graph(0, 1, 1))
                        wait_apart(sp)
                        sp.dma_start(x_now[:, :, :], of(x_tiles, k + 1)).then_inc(x_loaded, DMA)
                    stack_layer1(at, 2)
                if first >= 1:
                    sp.wait_ge(y_ready, at.graph(-1, 2, 2))
                    wait_apart(sp)
                    sp.dma_start(of(out_tiles, k - 1), y[:, :, :]).then_inc(y_stored, DMA)
                if has_this:
                    stack_layer1(at, 3)

            walk(sp, emit)
            sp.wait_ge(y_stored, DMA * graphs)

        @block.tensor
        def _(pe):
            def turn(dst, src):
                return nc.tensor.transpose(dst, src, ident[:, :])

            def take_bank(at, n):
                if n >= 2 or at.body.before is not None:
                    wait_out(pe, at, n - 2)
                return work_bank[at.bank_ring(n)]

            def project_features(dst, w, src, c):
                for i in range(DC):
                    last = nc.tensor.matmul(dst[:, :], w[:, i, c * P:(c + 1) * P], src[:, i, :],
                                            start=i == 0, stop=i == DC - 1)
                return last

            def project_tokens(dst, src, w, part):
                for t in range(2):
                    tile = (2 * part + t) * P
                    for i in range(DC):
                        last = nc.tensor.matmul(dst[:, t * dim:(t + 1) * dim], src[:, i, tile:tile + P], w[:, i, :],
                                                start=i == 0, stop=i == DC - 1)
                return last

            def turn_tokens(dst, c):
                for t in range(QT):
                    last = turn(dst[:, t * P:(t + 1) * P], tok[:, t, c * P:(c + 1) * P])
                return last

            def fill(at, n, s, task, ahead, part):
                dst = take_bank(at, n)
                if task == "fold":
                    if part == 0:
                        pe.wait_ge(blocks_loaded, DMA * HC1)
                        for i in range(DC):
                            for c in range(DC):
                                col = i * dim + c * P
                                last = nc.tensor.matmul(dst[:, col:col + P], gcn_raw[:, c, i * P:(i + 1) * P],
                                                        head_blocks[:, :], start=True, stop=True)
                    else:
                        pe.wait_ge(bias_widened, 1)
                        for c in range(DC):
                            last = nc.tensor.matmul(dst[:, c * P:(c + 1) * P], gcn_b_wide[:, c, :],
                                                    head_blocks[:, :], start=True, stop=True)
                elif task in ("h0_turn", "h1_turn"):
                    pe.wait_ge(normalised[int(task[1])], at.graph(ahead, 1, 1))
                    last = turn_tokens(dst, part)
                elif task == "v0":
                    wait_out(pe, at, at.latest(s, "h0_turn", 1))
                    last = project_tokens(dst, h_t, wv_sb, part)
                elif task in ("q0", "k0"):
                    wait_out(pe, at, at.latest(s, "h0_turn", 1))
                    last = project_features(dst, wq_sb if task == "q0" else wk_sb, h_t, part)
                elif task == "out_proj":
                    wait_out(pe, at, at.latest(s, "pv", 1, "X"))
                    last = project_tokens(dst, o_t, wo_sb, part)
                elif task == "m":
                    wait_out(pe, at, at.latest(s, "h1_turn", 1))
                    last = project_tokens(dst, h_t, map_sb, part)
                elif task == "m_turn":
                    wait_out(pe, at, at.latest(s, "m", 1))
                    last = turn_tokens(dst, part)
                elif task in ("q1", "k1"):
                    wait_out(pe, at, at.latest(s, "m_turn", 1))
                    last = project_features(dst, qw_sb if task == "q1" else kw_sb, m_t, part)
                elif task == "n_turn":
                    pe.wait_ge(n_ready, at.graph(ahead, 1, 1))
                    last = turn_tokens(dst, part)
                elif task == "finish":
                    wait_out(pe, at, at.latest(s, "pv", 3, "Y"))
                    for t in range(2):
                        tile = (2 * part + t) * P
                        for c in range(DC):
                            col = t * dim + c * P
                            last = turn(dst[:, col:col + P], o_t[:, c, tile:tile + P])
                else:
                    assert task == "v1"
                    if at.first == 0:
                        wait_out_of_fold(at)
                    last = project_tokens(dst, h_t, gcn_sb, part)
                last.then_inc(bank_filled, 1)

            def wait_out_of_fold(at):
                pe.wait_ge(bank_emptied["dve"], 2)

            def times_values(at, n, s, kind, group):
                dst = take_bank(at, n)
                pe.wait_ge(turn_copied, at.units(at.body.lagged_number(s, LAG_PV) + 1))
                if kind == "X":
                    wait_out(pe, at, at.latest(s, "v0", 1))
                    for c in range(QT):
                        for h in range(2):
                            col = (2 * group + h) * D0
                            last = nc.tensor.matmul(dst[D0 * h:D0 * h + D0, :], v0[:, c, col:col + D0],
                                                    prob_t_x[:, h, c, :], start=c == 0, stop=c == QT - 1,
                                                    skip_group_check=True)
                else:
                    if group == 0:
                        wait_out(pe, at, at.latest(s, "v1", 1))
                    for c in range(QT):
                        for j in range(HC1):
                            col = ((group // 2) * HC1 + j) * D1
                            last = nc.tensor.matmul(dst[D1 * j:D1 * j + D1, 0:HALF], v1[:, c, col:col + D1],
                                                    prob_t_y[:, j, c, :], start=c == 0, stop=c == QT - 1,
                                                    skip_group_check=True)
                last.then_inc(bank_filled, 1)

            def scores(at, s, kind, u):
                n = at.body.unit_number(s)
                if at.n_units + n >= 2:
                    pe.wait_ge(masked, at.units(n - 1))
                dst = score_bank[at.unit_ring(n, 2)]
                if kind == "X":
                    head, _, t = unit_x(u)
                    if u == 0:
                        pe.wait_ge(q0_stacked, at.graph(1, Q0_DMAS, Q0_DMAS))
                        pe.wait_ge(k0_stacked, at.graph(1, K0_DMAS, K0_DMAS))
                    q = q0_stack[:, head, t * P:(t + 1) * P]
                    nc.tensor.matmul(dst[:, :], q, k0_high[:, head, :], start=True, stop=False)
                    nc.tensor.matmul(dst[:, :], q, k0_low[:, head, :], start=False, stop=True).then_inc(scores_ready, 1)
                else:
                    head, j, t, _ = unit_y(u)
                    if u < GROUP and u % 2 == 0:
                        pe.wait_ge(stacked[j], at.graph(-1, STACK_DMAS, STACK_DMAS))
                    nc.tensor.matmul(dst[:, :], q1_stack[:, head, t * P:(t + 1) * P], k1_stack[:, head, :],
                                     start=True, stop=True).then_inc(scores_ready, 1)
                    if u >= 2:
                        pe.wait_ge(picked, at.graph(-1, Y_SLOTS, u - 1))
                    nc.tensor.matmul(cos_bank[u % 2][:, :], ns_stack[:, head, t * P:(t + 1) * P], nm_stack[:, head, :],
                                     start=True, stop=True).then_inc(cos_ready, 1)

            def turn_weights(at, s, kind, u):
                n = at.body.lagged_number(s, LAG_TURN)
                ahead = graph_ahead(s, LAG_TURN, kind)
                if kind == "X":
                    pe.wait_ge(normed, at.graph(ahead, X_SLOTS, u + 1))
                else:
                    pe.wait_ge(picked, at.graph(ahead, Y_SLOTS, u + 1))
                if at.n_units + n >= 2:
                    pe.wait_ge(turn_copied, at.units(n - 1))
                dst, r = turn_bank[at.unit_ring(n, 2)], at.unit_ring(n, 4)
                for c in range(QT):
                    last = turn(dst[:, c * P:(c + 1) * P], prob[:, r, c * P:(c + 1) * P])
                last.then_inc(turned, 1)

            pe.wait_ge(consts_made, 1)
            pe.wait_ge(weights_loaded, WEIGHT_DMAS)

            def emit(at):
                n = 0
                for s in range(N_SLOTS):
                    if at.body.units[s]:
                        scores(at, s, *at.body.units[s])
                    for task, ahead, part in at.body.tasks[s]:
                        if task == "pv":
                            times_values(at, n, s, ahead, part)
                            n += 1
                        elif task in PSUM_TASKS:
                            fill(at, n, s, task, ahead, part)
                            n += 1
                    if at.body.lagged(s, LAG_TURN):
                        turn_weights(at, s, *at.body.lagged(s, LAG_TURN))

            walk(pe, emit)

        @block.vector
        def _(dve):
            emptied = bank_emptied["dve"]

            def mask_and_max(at, s, kind, u):
                n = at.body.unit_number(s)
                dve.wait_ge(scores_ready, at.units(n + 1))
                if at.n_units + n >= 4:
                    dve.wait_ge(turned, at.units(n - 3))
                if kind == "X":
                    t, mask, scale = unit_x(u)[2], mask0, C0
                    if u == 0:
                        dve.wait_ge(masks_made, mask_number(at, 0))
                else:
                    t, mask, scale = unit_y(u)[2], mask1, C1
                    if u == 0:
                        dve.wait_ge(masks_made, at.graph(0, 2, 1 if at.first < graphs else 0))
                wait_apart(dve)
                r = at.unit_ring(n, 4)
                nc.vector.tensor_tensor_reduce(out=prob[:, r, :], in0=score_bank[at.unit_ring(n, 2)][:, :],
                                               in1=mask[:, t, :], scale=-scale, scalar=BIG, op0=ALU.add, op1=ALU.min,
                                               accum_out=row_min[:, r:r + 1]).then_inc(masked, 1)

            def select(at, s, kind, u):
                n = at.body.lagged_number(s, LAG_SELECT)
                dve.wait_ge(exped, at.units(n + 1))
                r = at.unit_ring(n, 4)
                if kind == "X":
                    nc.vector.reciprocal(inv0[:, u:u + 1], sum0[:, u:u + 1]).then_inc(inverted, 1)
                else:
                    head, _, t, _ = unit_y(u)
                    dve.wait_ge(cos_ready, at.graph(graph_ahead(s, LAG_SELECT, kind), Y_SLOTS, u + 1))
                    nc.vector.scalar_tensor_tensor(out=prob[:, r, :], in0=cos_bank[u % 2][:, :], scalar=COS_MIN,
                                                   in1=prob[:, r, :], op0=ALU.is_gt, op1=ALU.mult,
                                                   accum_out=picked1[:, t, head:head + 1]).then_inc(picked, 1)

            def row_stats(at, ahead, layer, src):
                for t in range(QT):
                    last = nc.vector.bn_stats(stats[:, t, :], src[:, t, :])
                last.then_inc(stats_taken[layer], 1)
                dve.wait_ge(stats_taken[layer], at.graph(ahead, 1, 1))
                if at.first + ahead >= 1:
                    dve.wait_ge(normalised[layer], at.graph(ahead, 1, 0))
                wait_apart(dve)
                for t in range(QT):
                    last = nc.vector.bn_aggr(mean_var[layer][:, t, :], stats[:, t, :])
                last.then_inc(stats_ready[layer], 1)

            def row_factors(at, ahead):
                dve.wait_ge(picked, at.graph(ahead, Y_SLOTS, Y_SLOTS))
                nc.vector.tensor_tensor(factor[:, :, :], sum1[:, :, :], picked1[:, :, :], ALU.add).then_inc(factor_step, 1)
                nc.vector.tensor_scalar(keep_row[:, :], mask1[:, :, 0], NEG1 / 2, None, ALU.is_gt).then_inc(factor_step, 1)
                dve.wait_ge(factor_step, at.graph(ahead, 3, 2))
                nc.vector.reciprocal(factor[:, :, :], factor[:, :, :]).then_inc(factor_step, 1)
                dve.wait_ge(factor_step, at.graph(ahead, 3, 3))
                nc.vector.tensor_tensor(factor[:, :, :], factor[:, :, :],
                                        keep_row[:, :].unsqueeze(2).broadcast_to([P, QT, H1]),
                                        ALU.mult).then_inc(factors_ready, 1)

            def empty(at, n, s, task, ahead, part):
                dve.wait_ge(bank_filled, at.banks(n + 1))
                src = work_bank[at.bank_ring(n)]
                src_tiles = src[:, :].rearrange("p (t d) -> p t d", t=2)
                pair = slice(2 * part, 2 * part + 2)
                if task == "fold":
                    if part == 0:
                        nc.vector.tensor_copy(gcn_sb[:, :, :], src_tiles).then_inc(emptied, 1)
                    else:
                        nc.vector.tensor_copy(gcn_b_row[:, :], src[:, 0:dim]).then_inc(emptied, 1)
                elif task == "out_proj":
                    dve.wait_ge(bo_added, at.graph(ahead, 1, 1))
                    nc.vector.tensor_tensor(x_now[:, pair, :], src_tiles, x_now[:, pair, :], ALU.add).then_inc(emptied, 1)
                elif task in ("m", "v1"):
                    if at.first == 0 and task == "v1":
                        dve.wait_ge(emptied, 2)
                    dst, bias = (tok, map_b_row) if task == "m" else (v1, gcn_b_row)
                    nc.vector.tensor_tensor(dst[:, pair, :], src_tiles,
                                            bias[:, :].unsqueeze(1).broadcast_to([P, 2, dim]), ALU.add).then_inc(emptied, 1)
                elif task == "finish":
                    dve.wait_ge(factors_ready, at.graph(ahead, 1, 1))
                    if at.first + ahead >= 1:
                        dve.wait_ge(y_stored, at.graph(ahead, DMA, 0))
                    heads = factor[:, pair, :].rearrange("p t h -> p (t h)").unsqueeze(2).broadcast_to([P, 2 * H1, D1])
                    y_heads = y[:, pair, :].rearrange("p t (h d) -> p (t h) d", h=H1)
                    nc.vector.tensor_tensor(y_heads, src[:, :].rearrange("p (h d) -> p h d", d=D1), heads,
                                            ALU.mult).then_inc(emptied, 1)
                    wait_out(dve, at, n)
                    dve.wait_ge(x1_copied, at.graph(ahead, 1, 1))
                    nc.vector.scalar_tensor_tensor(out=y[:, pair, :], in0=y[:, pair, :], scalar=0.0,
                                                   in1=x1_kept[:, pair, :], op0=ALU.max, op1=ALU.add).then_inc(y_ready, 1)
                else:
                    parts, bias = {"q0": (q_parts, None), "k0": (k_parts, None), "n_turn": (n_parts, None),
                                   "q1": (q_parts, q_b_col), "k1": (k_parts, k_b_col)}[task]
                    high, low = parts[:, 0, part, :], parts[:, 1, part, :].bitcast(F32R)
                    dve.wait_ge(high_ready[task], at.graph(ahead, DC, part + 1))
                    if bias is None:
                        nc.vector.tensor_tensor(low, src[:, :], high, ALU.subtract).then_inc(emptied, 1)
                    else:
                        nc.vector.scalar_tensor_tensor(out=low, in0=src[:, :], scalar=bias[:, part:part + 1], in1=high,
                                                       op0=ALU.add, op1=ALU.subtract).then_inc(emptied, 1)

            def step(at, s, task, ahead):
                if task == "ln0_stats":
                    dve.wait_ge(tok_loaded, at.graph(ahead, DMA, DMA))
                    row_stats(at, ahead, 0, tok)
                elif task == "ln1_stats":
                    wait_out(dve, at, at.latest(s, "out_proj", 1))
                    row_stats(at, ahead, 1, x_now)
                elif task == "m_sums":
                    dve.wait_ge(squared, at.graph(ahead, 1, 1))
                    if at.first + ahead >= 1:
                        dve.wait_ge(inv_norm_ready, at.graph(ahead, 1, 0))
                    squares = m_t[:, :, :].rearrange("p c n -> p (c n)").rearrange("p (a d) -> p a d", d=D1)
                    nc.vector.reduce_sum(norm2[:, :], squares, AX_X).then_inc(summed, 1)
                elif task == "row_factors":
                    row_factors(at, ahead)
                elif task == "keep_x1":
                    if at.first >= 1:
                        dve.wait_ge(y_ready, at.graph(-1, 2, 2))
                    nc.vector.tensor_copy(x1_kept[:, :, :], x_now[:, :, :]).then_inc(x1_copied, 1)

            dve.wait_ge(weights_loaded, WEIGHT_DMAS)
            nc.vector.tensor_copy(gcn_b_wide[:, :, :],
                                  gcn_b_col[:, :].unsqueeze(2).broadcast_to([P, DC, P])).then_inc(bias_widened, 1)

            def emit(at):
                n = 0
                for s in range(N_SLOTS):
                    if at.body.units[s]:
                        mask_and_max(at, s, *at.body.units[s])
                    if at.body.lagged(s, LAG_SELECT):
                        select(at, s, *at.body.lagged(s, LAG_SELECT))
                    for task, ahead, part in at.body.tasks[s]:
                        if task in PSUM_TASKS:
                            if PSUM_TASKS[task] == "dve":
                                empty(at, n, s, task, ahead, part)
                            n += 1
                        else:
                            step(at, s, task, ahead)

            walk(dve, emit)

        @block.scalar
        def _(act):
            emptied = bank_emptied["act"]

            def exp(at, s, kind, u):
                n = at.body.unit_number(s)
                act.wait_ge(masked, at.units(n + 1))
                r = at.unit_ring(n, 4)
                if kind == "X":
                    total = sum0[:, u:u + 1]
                else:
                    head, _, t, _ = unit_y(u)
                    total = sum1[:, t, head:head + 1]
                nc.scalar.activation(prob[:, r, :], prob[:, r, :], ACT.Exp, bias=row_min[:, r:r + 1], scale=-1.0,
                                     accum_out=total).then_inc(exped, 1)

            def copy_turned(at, s, kind, u):
                n = at.body.lagged_number(s, LAG_TURN)
                act.wait_ge(turned, at.units(n + 1))
                if u % GROUP == 0 and at.n_units + n >= GROUP:
                    act.wait_ge(bank_filled, at.banks(at.latest(s, "pv") + 1))
                src = turn_bank[at.unit_ring(n, 2)][:, :].rearrange("p (c q) -> p c q", c=QT)
                if kind == "X":
                    _, h, t = unit_x(u)
                    dst = prob_t_x[:, h, :, t * P:(t + 1) * P]
                else:
                    _, j, _, q2 = unit_y(u)
                    dst = prob_t_y[:, j, :, q2 * P:(q2 + 1) * P]
                nc.scalar.copy(dst, src).then_inc(turn_copied, 1)

            def empty(at, n, s, task, ahead, part):
                if task in ("fold", "out_proj", "m", "v1", "finish"):
                    return
                act.wait_ge(bank_filled, at.banks(n + 1))
                src = work_bank[at.bank_ring(n)]
                if task == "pv":
                    if ahead == "X":
                        nc.scalar.copy(o_t[:, part, :], src[:, :]).then_inc(emptied, 1)
                    else:
                        half = (part % 2) * HALF
                        nc.scalar.copy(o_t[:, part // 2, half:half + HALF], src[:, 0:HALF]).then_inc(emptied, 1)
                elif task in ("h0_turn", "h1_turn"):
                    nc.scalar.activation(h_t[:, part, :], src[:, :], ACT.Relu).then_inc(emptied, 1)
                elif task == "v0":
                    nc.scalar.copy(v0[:, 2 * part:2 * part + 2, :],
                                   src[:, :].rearrange("p (t d) -> p t d", t=2)).then_inc(emptied, 1)
                elif task == "m_turn":
                    if part == 0:
                        act.wait_ge(summed, at.graph(ahead, 1, 1))
                    nc.scalar.copy(m_t[:, part, :], src[:, :]).then_inc(emptied, 1)
                else:
                    if part == 0 and task in ("q0", "k0", "n_turn") and at.first >= 1:
                        for j in range(HC1):
                            act.wait_ge(stacked[j], at.graph(0, STACK_DMAS, 0))
                    if part == 0 and task in ("q1", "k1"):
                        latest = 1 if at.first + 1 < graphs else 0
                        if task == "q1":
                            act.wait_ge(q0_stacked, at.graph(latest, Q0_DMAS, Q0_DMAS))
                        else:
                            act.wait_ge(k0_stacked, at.graph(latest, K0_DMAS, K0_DMAS))
                    parts, bias = {"q0": (q_parts, None), "k0": (k_parts, None), "n_turn": (n_parts, None),
                                   "q1": (q_parts, q_b_col), "k1": (k_parts, k_b_col)}[task]
                    high = parts[:, 0, part, :].bitcast(F32R)
                    if bias is None:
                        nc.scalar.activation(high, src[:, :], ACT.Identity).then_inc(high_ready[task], 1)
                    else:
                        nc.scalar.activation(high, src[:, :], ACT.Identity,
                                             bias=bias[:, part:part + 1]).then_inc(high_ready[task], 1)

            act.wait_ge(weights_loaded, WEIGHT_DMAS)

            def emit(at):
                n = 0
                for s in range(N_SLOTS):
                    if at.body.units[s]:
                        exp(at, s, *at.body.units[s])
                    for task, ahead, part in at.body.tasks[s]:
                        if task in PSUM_TASKS:
                            empty(at, n, s, task, ahead, part)
                            n += 1
                        elif task == "m_square":
                            wait_out(act, at, at.latest(s, "m", 1))
                            nc.scalar.activation(m_t[:, :, :].rearrange("p c n -> p (c n)"),
                                                 tok[:, :, :].rearrange("p t d -> p (t d)"),
                                                 ACT.Square).then_inc(squared, 1)
                    if at.body.lagged(s, LAG_TURN):
                        copy_turned(at, s, *at.body.lagged(s, LAG_TURN))

            walk(act, emit)

        @block.gpsimd
        def _(pool):
            def normalise(at, ahead, layer, src):
                pool.wait_ge(stats_ready[layer], at.graph(ahead, 1, 1))
                wait_apart(pool)
                nc.gpsimd.tensor_scalar(minus_mean[:, :], mean_var[layer][:, :, 0], -1.0, 0.0,
                                        ALU.mult, ALU.add).then_inc(norm_step[layer], 1)
                nc.gpsimd.tensor_scalar(var_eps[:, :], mean_var[layer][:, :, 1], LN_EPS, 1.0,
                                        ALU.add, ALU.mult).then_inc(norm_step[layer], 1)
                pool.wait_ge(norm_step[layer], at.graph(ahead, 3, 2))
                nc.gpsimd.tensor_tensor(rstd[:, :], var_eps[:, :], minus_half[:, 0:QT], ALU.pow).then_inc(norm_step[layer], 1)
                pool.wait_ge(norm_step[layer], at.graph(ahead, 3, 3))
                wait_apart(pool)
                for t in range(QT):
                    last = nc.gpsimd.tensor_scalar(tok[:, t, :], src[:, t, :], minus_mean[:, t:t + 1], rstd[:, t:t + 1],
                                                   ALU.add, ALU.mult)
                last.then_inc(normalised[layer], 1)

            def make_mask(at, layer):
                number = mask_number(at, layer)
                pool.wait_ge(adj_loaded, number * DMA)
                if layer == 0:
                    if at.body.before is not None:
                        pool.wait_ge(masked, at.units(0))
                    wait_apart(pool)
                    nc.gpsimd.tensor_scalar(mask0[:, :, :], adj_raw[:, :, :], -1.0, -NEG0,
                                            ALU.add, ALU.mult).then_inc(masks_made, 1)
                else:
                    if at.first >= 1:
                        pool.wait_ge(factors_ready, at.graph(0, 1, 0))
                    wait_apart(pool)
                    nc.gpsimd.tensor_scalar(mask1[:, :, :], adj_raw[:, :, :], NEG1, 0.0,
                                            ALU.mult, ALU.add).then_inc(masks_made, 1)

            def step(at, s, task, ahead):
                if task == "ln0_apply":
                    normalise(at, ahead, 0, tok)
                elif task == "ln1_apply":
                    wait_out(pool, at, at.latest(s, "h0_turn", 1))
                    normalise(at, ahead, 1, x_now)
                elif task == "add_bo":
                    pool.wait_ge(x_loaded, at.graph(ahead, DMA, DMA))
                    nc.gpsimd.tensor_tensor(x_now[:, :, :], x_now[:, :, :],
                                            bo_row[:, :].unsqueeze(1).broadcast_to([P, QT, dim]),
                                            ALU.add).then_inc(bo_added, 1)
                elif task in ("mask0", "mask1"):
                    make_mask(at, int(task[-1]))
                elif task == "m_norms":
                    pool.wait_ge(summed, at.graph(ahead, 1, 1))
                    wait_apart(pool)
                    nc.gpsimd.tensor_scalar(floored[:, :], norm2[:, :], NORM_FLOOR, BIG,
                                            ALU.max, ALU.min).then_inc(norms_floored, 1)
                    pool.wait_ge(norms_floored, at.graph(ahead, 1, 1))
                    nc.gpsimd.tensor_tensor(inv_norm[:, :], floored[:, :], minus_half[:, :], ALU.pow).then_inc(inv_norm_ready, 1)
                elif task == "n_scale":
                    wait_out(pool, at, at.latest(s, "m_turn", 1))
                    pool.wait_ge(inv_norm_ready, at.graph(ahead, 1, 1))
                    heads = tok[:, :, :].rearrange("p t d -> p (t d)").rearrange("p (a d) -> p a d", d=D1)
                    nc.gpsimd.tensor_tensor(heads, heads, inv_norm[:, :].unsqueeze(2).broadcast_to([P, QT * H1, D1]),
                                            ALU.mult).then_inc(n_ready, 1)

            nc.gpsimd.memset(head_blocks[:, :], 0.0).then_inc(blocks_zeroed, 1)
            nc.gpsimd.memset(minus_half[:, :], -0.5)
            nc.gpsimd.memset(ident[:, :], 0.0).then_inc(ident_zeroed, 1)
            pool.wait_ge(ident_zeroed, 1)
            nc.gpsimd.affine_select(out=ident[:, :], in_=ident[:, :], compare_op=ALU.not_equal, fill=1.0, base=0,
                                    pattern=[[-1, P]], channel_multiplier=1).then_inc(consts_made, 1)
            pool.wait_ge(consts_made, 1)
            pool.wait_ge(weights_loaded, WEIGHT_DMAS)

            def emit(at):
                for s in range(N_SLOTS):
                    done = at.body.lagged(s, LAG_SELECT)
                    if done and done[0] == "X":
                        u, r = done[1], at.unit_ring(at.body.lagged_number(s, LAG_SELECT), 4)
                        pool.wait_ge(inverted, at.graph(graph_ahead(s, LAG_SELECT, "X"), X_SLOTS, u + 1))
                        wait_apart(pool)
                        nc.gpsimd.tensor_scalar(prob[:, r, :], prob[:, r, :], inv0[:, u:u + 1], 1.0,
                                                ALU.mult, ALU.mult).then_inc(normed, 1)
                    for task, ahead, _ in at.body.tasks[s]:
                        if task not in PSUM_TASKS:
                            step(at, s, task, ahead)

            walk(pool, emit)


_OUT_SHAPE = (16, 512, 256)


def kernel(**inputs):
    import numpy as np
    import concourse.bacc as bacc
    from concourse.bass_utils import run_bass_kernel_spmd

    def laid(name, turned=False):
        a = np.asarray(inputs[name])
        return np.ascontiguousarray(a.T if turned else a)

    def column(name):
        return np.ascontiguousarray(np.asarray(inputs[name]).reshape(-1, P).T)

    arrays = {
        "x": laid("x"), "adj": laid("adj"),
        "wq": laid("L0_gnn_Wq"), "wk": laid("L0_gnn_Wk"), "wv": laid("L0_gnn_Wv"), "wo": laid("L0_gnn_Wo"),
        "bo": laid("L0_gnn_bo"),
        "map_w": laid("L1_gnn_map_w", True), "map_b": laid("L1_gnn_map_b"),
        "q_w": laid("L1_gnn_q_w", True), "q_b": column("L1_gnn_q_b"),
        "k_w": laid("L1_gnn_k_w", True), "k_b": column("L1_gnn_k_b"),
        "gcn_w": laid("L1_gnn_gcn_map_w"), "gcn_b": column("L1_gnn_gcn_map_b"),
        "gcn_head_w": laid("L1_gnn_gcn_W", True),
    }
    nc = bacc.Bacc("TRN2", target_bir_lowering=False, num_devices=1)
    args = [nc.dram_tensor(f"{n}_dram", a.shape, mybir.dt.from_np(a.dtype), kind="ExternalInput").ap()
            for n, a in arrays.items()]
    out = nc.dram_tensor("out_dram", _OUT_SHAPE, F32, kind="ExternalOutput").ap()
    attention_layers(nc, *args, out)
    r = run_bass_kernel_spmd(nc, [{f"{n}_dram": a for n, a in arrays.items()}], core_ids=[0])
    return r.results[0]["out_dram"]
```

```python
from contextlib import ExitStack

import concourse.bass as bass
from concourse import mybir

F32 = mybir.dt.float32
F32R = mybir.dt.float32r
BF16 = mybir.dt.bfloat16
U8 = mybir.dt.uint8
ALU = mybir.AluOpType
ACT = mybir.ActivationFunctionType
AX_X = mybir.AxisListType.X

P = 128
BANK = 512
NEG0 = -3.3895e38
NEG1 = -1e10
LN_EPS = 1e-5
NORM_FLOOR = 1e-16
COS_MIN = 0.1
BIG = 3.4e38

Y_SLOTS, X_SLOTS = 32, 16
N_SLOTS = Y_SLOTS + X_SLOTS
GROUP = 8
TURN_RING = 12
LAG_COS, LAG_SELECT, LAG_TURN, LAG_PV = 1, 1, 3, 4

SLOTS = {
    0: [("q0", 1, 0)], 1: [("q0", 1, 1), ("add_bo", 0, 0)],
    2: [("k0", 1, 0), ("mask0", 1, 0)], 4: [("k0", 1, 1)],
    5: [("v0", 1, 0)], 6: [("out_proj", 0, 0)], 7: [("out_proj", 0, 1)], 8: [("v0", 1, 1)],
    9: [("ln1_stats", 0, 0), ("ln1_apply", 0, 0)],
    13: [("h1_turn", 0, 0)], 14: [("h1_turn", 0, 1)],
    16: [("m", 0, 0)], 17: [("m", 0, 1)],
    18: [("m_square", 0, 0)], 19: [("m_square", 0, 1)], 20: [("m_sums", 0, 0), ("m_norms", 0, 0)],
    21: [("m_turn", 0, 0)], 22: [("m_turn", 0, 1)],
    23: [("q1", 0, 0)], 24: [("q1", 0, 1), ("n_scale", 0, 0)], 25: [("k1", 0, 0)], 26: [("k1", 0, 1)],
    29: [("n_turn", 0, 0)], 30: [("n_turn", 0, 1)],
    33: [("row_factors", -1, 0)],
    34: [("mask1", 0, 0), ("ln0_stats", 2, 0)], 35: [("ln0_apply", 2, 0)],
    37: [("finish", -1, 0)], 38: [("finish", -1, 1), ("v1", 0, 0)], 39: [("v1", 0, 1)],
    41: [("h0_turn", 2, 0)], 42: [("h0_turn", 2, 1)],
    45: [("keep_x1", 0, 0)],
}
FIRST_SLOT = [("ln0_stats", 1, 0), ("ln0_apply", 1, 0), ("fold", 0, 0), ("fold", 0, 1),
              ("h0_turn", 1, 0), ("h0_turn", 1, 1)]
PSUM_TASKS = {"h0_turn": "act", "v0": "act", "out_proj": "dve", "q0": "dve", "k0": "dve",
              "h1_turn": "act", "m": "dve", "m_turn": "act", "q1": "dve", "k1": "dve",
              "n_turn": "dve", "finish": "dve", "v1": "dve", "fold": "dve", "pv": "act"}
TWO_PIECES = ("v0", "out_proj", "q0", "k0", "m", "q1", "k1", "v1", "pv")


class Body:

    def __init__(self, k, graphs, before):
        self.units = [None] * N_SLOTS
        if k >= 1:
            self.units[:Y_SLOTS] = [("Y", u) for u in range(Y_SLOTS)]
        if k + 1 < graphs:
            self.units[Y_SLOTS:] = [("X", u) for u in range(X_SLOTS)]
        self.before = before
        self.tasks = []
        self.last = 0
        for s in range(N_SLOTS):
            here = list(FIRST_SLOT) if k == -1 and s == 0 else []
            for task, ahead, part in SLOTS.get(s, []):
                if 0 <= k + ahead < graphs:
                    here.append((task, ahead, part))
            done = self.lagged(s, LAG_PV)
            if done and done[1] % GROUP == GROUP - 1:
                here.append(("pv", done[0], done[1] // GROUP))
            self.tasks.append(here)
        self.bank_tasks = [(s, t) for s, here in enumerate(self.tasks) for t in here if t[0] in PSUM_TASKS]
        self.pieces = [[] for _ in range(N_SLOTS)]
        self.emptying = [[] for _ in range(N_SLOTS)]
        for n, (s, t) in enumerate(self.bank_tasks):
            count = 2 if t[0] in TWO_PIECES else 1
            for piece in range(count):
                self.pieces[s + piece].append((n, s, piece, piece == count - 1))
            self.emptying[s + count].append(n)
        ended = [n for s in range(N_SLOTS) for n, _, _, last in self.pieces[s] if last]
        assert ended == sorted(ended)
        self.n_units = sum(u is not None for u in self.units)

    def lagged(self, s, lag):
        if s >= lag:
            return self.units[s - lag]
        return self.before.units[N_SLOTS + s - lag] if self.before else None

    def unit_number(self, s):
        return sum(u is not None for u in self.units[:s])

    def lagged_number(self, s, lag):
        if s >= lag:
            return self.unit_number(s - lag)
        return self.before.unit_number(N_SLOTS + s - lag) - self.before.n_units

    def emptied(self, engine):
        return sum(PSUM_TASKS[t[0]] == engine for _, t in self.bank_tasks)


class At:

    def __init__(self, k, body, units, banks, emptied, first=None, step=None):
        self.k, self.body = k, body
        self.first = k if first is None else first
        self.n_units, self.n_banks, self.n_emptied, self.step = units, banks, emptied, step

    def _passes(self, value, per_pass):
        return value if self.step is None else (self.k - self.first) * per_pass + value

    def units(self, n):
        return self._passes(self.n_units + n, self.step and self.step[0])

    def unit_ring(self, n, size):
        return (self.n_units + n) % size

    def banks(self, n):
        return self._passes(self.n_banks + n, self.step and self.step[1])

    def bank_ring(self, n):
        return (self.n_banks + n) % 2

    def _emptied(self, engine, n):
        return self._passes(self.n_emptied[engine] + n, self.step and self.step[2][engine])

    def emptied(self, i):
        tasks = self.body.bank_tasks if i >= 0 else self.body.before.bank_tasks
        engine = PSUM_TASKS[tasks[i][1][0]]
        if i >= 0:
            return engine, self._emptied(engine, sum(PSUM_TASKS[t[0]] == engine for _, t in tasks[:i + 1]))
        return engine, self._emptied(engine, 1 - sum(PSUM_TASKS[t[0]] == engine for _, t in tasks[i:]))

    def latest(self, s, task, part=None, which=None):
        def found(tasks, until):
            return [i for i, (at, t) in enumerate(tasks)
                    if at <= until and t[0] == task and part in (None, t[2]) and which in (None, t[1])]
        here = found(self.body.bank_tasks, s)
        if here:
            return here[-1]
        before = self.body.before.bank_tasks
        return found(before, N_SLOTS)[-1] - len(before)

    def graph(self, ahead, each, plus):
        return (self.k + ahead) * each + plus


def attention_layers(nc, x, adj, wq, wk, wv, wo, bo, map_w, map_b, q_w, q_b, k_w, k_b,
                     gcn_w, gcn_b, gcn_head_w, out):
    graphs, tokens, dim = x.shape
    QT = tokens // P
    DC = dim // P
    H0, H1 = 4, 8
    D0, D1 = dim // H0, dim // H1
    HC0, HC1 = H0 // DC, H1 // DC
    HALF = tokens // 2
    C0, C1 = float(D0) ** -0.5, float(D1) ** -0.5
    DMA = 16
    FOLD_DMAS, LATER_DMAS = 2 * DMA, 8 * DMA
    STACK0_DMAS = 2 * HC0 * DMA
    STACK1_DMAS = 2 * HC1 * DMA
    assert (QT, DC, D0, D1, tokens) == (4, 2, 64, 32, BANK)

    body_first = Body(-1, graphs, None)
    body_0 = Body(0, graphs, body_first)
    body_loop = Body(1, graphs, body_0)
    body_14 = Body(graphs - 2, graphs, body_loop)
    body_15 = Body(graphs - 1, graphs, body_14)
    body_16 = Body(graphs, graphs, body_15)
    LOOP_FROM, LOOP_TO = 1, graphs - 2
    ats, units, banks, emptied = {}, 0, 0, {"act": 0, "dve": 0}
    for name, k, body, passes in (("first", -1, body_first, 1), ("0", 0, body_0, 1),
                                  ("loop", 1, body_loop, LOOP_TO - LOOP_FROM),
                                  ("14", graphs - 2, body_14, 1), ("15", graphs - 1, body_15, 1),
                                  ("16", graphs, body_16, 1)):
        ats[name] = (k, body, units, banks, dict(emptied))
        units += passes * body.n_units
        banks += passes * len(body.bank_tasks)
        for e in emptied:
            emptied[e] += passes * body.emptied(e)
    loop_step = (body_loop.n_units, len(body_loop.bank_tasks), {e: body_loop.emptied(e) for e in emptied})
    assert loop_step[0] % 4 == loop_step[0] % TURN_RING == 0 and loop_step[1] % 2 == 0
    tail = [[t for s, t in b.bank_tasks if (s, t[0]) > (Y_SLOTS + 6, "finish")] for b in (body_0, body_loop)]
    assert tail[0] == tail[1], tail

    def walk(engine, emit):
        for name in ("first", "0"):
            emit(At(*ats[name]))
        with engine.Fori(LOOP_FROM, LOOP_TO) as k:
            emit(At(k, *ats["loop"][1:], first=LOOP_FROM, step=loop_step))
        for name in ("14", "15", "16"):
            emit(At(*ats[name]))

    ctx = ExitStack()
    with ctx:
        def sb(name, shape, dt=F32):
            return ctx.enter_context(nc.sbuf_tensor(name, shape, dt))

        def sem(name):
            return ctx.enter_context(nc.semaphore(name))

        wq_sb, wk_sb, wv_sb, wo_sb = (sb(n, [P, DC, dim]) for n in ("wq_sb", "wk_sb", "wv_sb", "wo_sb"))
        map_sb, qw_sb, kw_sb = (sb(n, [P, DC, dim]) for n in ("map_sb", "qw_sb", "kw_sb"))
        gcn_sb = sb("gcn_sb", [P, DC, dim])
        gcn_b_col = sb("gcn_b_col", [P, DC])
        bo_row, map_b_row, gcn_b_row = (sb(n, [P, dim]) for n in ("bo_row", "map_b_row", "gcn_b_row"))
        q_b_col, k_b_col = sb("q_b_col", [P, DC]), sb("k_b_col", [P, DC])
        ident = sb("ident", [P, P])
        minus_half = sb("minus_half", [P, QT * H1])
        q0_stack = sb("q0_stack", [P, H0, tokens], F32R)
        k0_stacks = sb("k0_stacks", [P, H0, 2, tokens], F32R)
        k0_high, k0_low = k0_stacks[:, :, 0], k0_stacks[:, :, 1]
        stationary_stacks = sb("stationary_stacks", [P, 2, H1, tokens], F32R)
        q1_stack, ns_stack = stationary_stacks[:, 0], stationary_stacks[:, 1]
        moving_stacks = sb("moving_stacks", [P, 2, H1, tokens], F32R)
        nm_stack, k1_stack = moving_stacks[:, 0], moving_stacks[:, 1]
        parts = sb("parts", [P, 3, DC, 2, tokens])
        q_parts, n_parts, k_parts = parts[:, 0], parts[:, 1], parts[:, 2]
        h_t = sb("h_t", [P, DC, tokens])
        tok = sb("tok", [P, QT, dim])
        m_t = sb("m_t", [P, DC, tokens])
        v0, v1 = sb("v0_sb", [P, QT, dim]), sb("v1_sb", [P, QT, dim])
        x_now = sb("x_now", [P, QT, dim])
        x1_kept = sb("x1_kept", [P, QT, dim])
        head_blocks = x1_kept[:, 0, 0:P]
        gcn_b_wide = x1_kept[:, 1].rearrange("p (c q) -> p c q", c=DC)
        o_t = sb("o_t", [P, DC, tokens])
        adj_raw = sb("adj_raw", [P, QT, tokens], U8)
        mask0, mask1 = sb("mask0_sb", [P, QT, tokens], BF16), sb("mask1_sb", [P, QT, tokens], BF16)
        prob = sb("prob", [P, 4, tokens])
        prob_t = sb("prob_t", [P, TURN_RING, QT, P])
        gcn_raw = prob_t[:, 0:DC * dim // BANK].rearrange("p u c q -> p (u c q)").rearrange("p (c n) -> p c n", c=DC)
        row_min = sb("row_min", [P, 4])
        sum0, inv0 = sb("sum0", [P, X_SLOTS]), sb("inv0", [P, X_SLOTS])
        sum1, picked1 = sb("sum1", [P, QT, H1]), sb("picked1", [P, QT, H1])
        factor, keep_row = sb("factor", [P, QT, H1]), sb("keep_row", [P, QT])
        stats = sb("stats", [P, QT, 6])
        mean_var = [sb("mean_var0", [P, QT, 2]), sb("mean_var1", [P, QT, 2])]
        minus_mean, var_eps, rstd = sb("minus_mean", [P, QT]), sb("var_eps", [P, QT]), sb("rstd", [P, QT])
        norm2, floored, inv_norm = (sb(n, [P, QT * H1]) for n in ("norm2", "floored", "inv_norm"))

        def bank(name):
            return ctx.enter_context(nc.psum_tensor(name, [P, BANK], F32))

        score_bank = [bank("score0"), bank("score1")]
        cos_bank = [bank("cos0"), bank("cos1")]
        turn_bank = [bank("turn0"), bank("turn1")]
        work_bank = [bank("work0"), bank("work1")]

        fold_loaded, blocks_zeroed, blocks_loaded = sem("fold_loaded"), sem("blocks_zeroed"), sem("blocks_loaded")
        wq_loaded, wk_loaded, wv_loaded = sem("wq_loaded"), sem("wk_loaded"), sem("wv_loaded")
        later_loaded = sem("later_loaded")
        ident_zeroed, consts_made, bias_widened = sem("ident_zeroed"), sem("consts_made"), sem("bias_widened")
        waits_passed = sem("waits_passed")
        scores_ready, masked, exped, turned, turn_copied = (
            sem(n) for n in ("scores_ready", "masked", "exped", "turned", "turn_copied"))
        inverted, normed = sem("inverted"), sem("normed")
        cos_ready, picked = sem("cos_ready"), sem("picked")
        bank_filled = sem("bank_filled")
        bank_emptied = {"act": sem("bank_emptied_act"), "dve": sem("bank_emptied_dve")}
        tok_loaded, x_loaded, adj_loaded, y_stored = (
            sem(n) for n in ("tok_loaded", "x_loaded", "adj_loaded", "y_stored"))
        stats_taken = [sem("stats0_taken"), sem("stats1_taken")]
        stats_ready = [sem("stats0_ready"), sem("stats1_ready")]
        norm_step = [sem("norm0_step"), sem("norm1_step")]
        normalised = [sem("normalised0"), sem("normalised1")]
        high_ready = {n: sem(n + "_high_ready") for n in ("q0", "k0", "q1", "k1", "n_turn")}
        q0_stacked, k0_stacked = sem("q0_stacked"), sem("k0_stacked")
        stacked = [sem(f"stacked{j}") for j in range(HC1)]
        bo_added, x1_copied = sem("bo_added"), sem("x1_copied")
        masks_made = sem("masks_made")
        squared, summed, norms_floored, inv_norm_ready, n_ready = (
            sem(n) for n in ("squared", "summed", "norms_floored", "inv_norm_ready", "n_ready"))
        factor_step, factors_ready, scaled = sem("factor_step"), sem("factors_ready"), sem("scaled")

        def unit_x(u):
            pair, rest = divmod(u, GROUP)
            h, t = divmod(rest, QT)
            return pair * 2 + h, h, t

        def unit_y(u):
            group, rest = divmod(u, GROUP)
            j, q2 = divmod(rest, 2)
            return (group // 2) * HC1 + j, j, (group % 2) * 2 + q2, q2

        def graph_ahead(s, lag, kind):
            return {"X": 1, "Y": -1}[kind] - (1 if s < lag else 0)

        def mask_number(at, layer):
            if at.first < 0:
                return 1
            return at.graph(0, 2, 2 + (layer if at.first + 1 < graphs else 0))

        def wait_out(eng, at, i):
            engine, count = at.emptied(i)
            eng.wait_ge(bank_emptied[engine], count)

        def wait_apart(eng):
            eng.sem_inc(waits_passed, 1)

        block = ctx.enter_context(nc.Block())

        @block.sync
        def _(sp):
            x_tiles = x.rearrange("b (t p) d -> b p t d", p=P)
            out_tiles = out.rearrange("b (t p) d -> b p t d", p=P)
            adj_tiles = adj.rearrange("b (t p) k -> b p t k", p=P)

            def of(tiles, g):
                return tiles[bass.ds(g, 1)].rearrange("a p t d -> (a p) t d")

            def stack_layer0(at):
                wait_out(sp, at, at.latest(N_SLOTS, "q0", 1))
                wait_apart(sp)
                if at.first >= 0:
                    sp.wait_ge(normed, at.graph(1, X_SLOTS, 0))
                for j in range(HC0):
                    for g in range(2):
                        sp.dma_start(q0_stack[D0 * g:D0 * g + D0, j:H0:HC0, :].bitcast(F32),
                                     q_parts[D0 * j:D0 * j + D0, :, g, :]).then_inc(q0_stacked, DMA)
                wait_out(sp, at, at.latest(N_SLOTS, "k0", 1))
                for j in range(HC0):
                    for g in range(2):
                        sp.dma_start(k0_stacks[D0 * g:D0 * g + D0, j:H0:HC0, :, :].bitcast(F32),
                                     k_parts[D0 * j:D0 * j + D0, :, :, :]).then_inc(k0_stacked, DMA)

            def stack_layer1(at, j):
                if at.first >= 1:
                    sp.wait_ge(cos_ready, at.graph(-1, Y_SLOTS, 3 * GROUP + 2 * j + 2))
                for dst, src, rows in ((stationary_stacks, parts[:, 0:2], (0, 0, 1, 1)),
                                       (moving_stacks, parts[:, 1:3], (0, 1, 0, 1))):
                    for g, which in enumerate(rows):
                        sp.dma_start(dst[D1 * g:D1 * g + D1, :, j:H1:HC1, :].bitcast(F32),
                                     src[D1 * j:D1 * j + D1, :, :, which, :]).then_inc(stacked[j], DMA)

            def load_adj(at, ahead, layer):
                if at.first >= 0:
                    sp.wait_ge(masks_made, mask_number(at, layer) - 1)
                wait_apart(sp)
                sp.dma_start(adj_raw[:, :, :], of(adj_tiles, at.k + ahead)).then_inc(adj_loaded, DMA)

            sp.dma_start(tok[:, :, :], of(x_tiles, 0)).then_inc(tok_loaded, DMA)
            sp.dma_start(gcn_raw, gcn_w.rearrange("(c p) n -> p c n", p=P)).then_inc(fold_loaded, DMA)
            sp.dma_start(gcn_b_col[:, :], gcn_b).then_inc(fold_loaded, DMA)
            sp.wait_ge(blocks_zeroed, 1)
            for g in range(HC1):
                sp.dma_start(head_blocks[D1 * g:D1 * g + D1, D1 * g:D1 * g + D1], gcn_head_w).then_inc(blocks_loaded, DMA)
            for dst, src, loaded in ((wq_sb, wq, wq_loaded), (wk_sb, wk, wk_loaded), (wv_sb, wv, wv_loaded)):
                sp.dma_start(dst[:, :, :], src.rearrange("(c p) n -> p c n", p=P)).then_inc(loaded, DMA)

            def load_later():
                for dst, src in ((wo_sb, wo), (map_sb, map_w), (qw_sb, q_w), (kw_sb, k_w)):
                    sp.dma_start(dst[:, :, :], src.rearrange("(c p) n -> p c n", p=P)).then_inc(later_loaded, DMA)
                for dst, src in ((q_b_col, q_b), (k_b_col, k_b)):
                    sp.dma_start(dst[:, :], src).then_inc(later_loaded, DMA)
                for dst, src in ((bo_row, bo), (map_b_row, map_b)):
                    sp.dma_start(dst[:, :], src.partition_broadcast(P)).then_inc(later_loaded, DMA)
                sp.dma_start(x_now[:, :, :], of(x_tiles, 0)).then_inc(x_loaded, DMA)

            def emit(at):
                first, k = at.first, at.k
                has_next, has_this = first + 1 < graphs, 0 <= first < graphs
                if has_next:
                    load_adj(at, 1, 0)
                if first < 0:
                    wait_out(sp, at, at.latest(0, "h0_turn", 1))
                    sp.dma_start(tok[:, :, :], of(x_tiles, k + 2)).then_inc(tok_loaded, DMA)
                if has_next:
                    stack_layer0(at)
                if first < 0:
                    load_later()
                if has_this:
                    load_adj(at, 0, 1)
                    wait_out(sp, at, at.latest(N_SLOTS, "n_turn", 1))
                    if first + 2 < graphs:
                        wait_apart(sp)
                        sp.dma_start(tok[:, :, :], of(x_tiles, k + 2)).then_inc(tok_loaded, DMA)
                    for j in range(HC1 - 1):
                        stack_layer1(at, j)
                if first >= 1:
                    wait_out(sp, at, at.latest(N_SLOTS, "finish", 1))
                    wait_apart(sp)
                    sp.dma_start(of(out_tiles, k - 1), x1_kept[:, :, :]).then_inc(y_stored, DMA)
                if has_this:
                    stack_layer1(at, HC1 - 1)
                    if has_next:
                        sp.wait_ge(x1_copied, at.graph(0, 1, 1))
                        wait_apart(sp)
                        sp.dma_start(x_now[:, :, :], of(x_tiles, k + 1)).then_inc(x_loaded, DMA)

            walk(sp, emit)
            sp.wait_ge(y_stored, DMA * graphs)

        @block.tensor
        def _(pe):
            def turn(dst, src):
                return nc.tensor.transpose(dst, src, ident[:, :])

            def take_bank(at, n):
                if n >= 2 or at.body.before is not None:
                    wait_out(pe, at, n - 2)
                return work_bank[at.bank_ring(n)]

            def project_features(dst, w, src, c, i):
                return nc.tensor.matmul(dst[:, :], w[:, i, c * P:(c + 1) * P], src[:, i, :],
                                        start=i == 0, stop=i == DC - 1)

            def project_tokens(dst, src, w, part, t):
                tile = (2 * part + t) * P
                for i in range(DC):
                    last = nc.tensor.matmul(dst[:, t * dim:(t + 1) * dim], src[:, i, tile:tile + P], w[:, i, :],
                                            start=i == 0, stop=i == DC - 1)
                return last

            def turn_tokens(dst, c):
                for t in range(QT):
                    last = turn(dst[:, t * P:(t + 1) * P], tok[:, t, c * P:(c + 1) * P])
                return last

            def await_operands(at, s, task, ahead, part):
                if task == "fold":
                    if part == 0:
                        pe.wait_ge(fold_loaded, FOLD_DMAS)
                        pe.wait_ge(blocks_loaded, DMA * HC1)
                    else:
                        pe.wait_ge(bias_widened, 1)
                elif task in ("h0_turn", "h1_turn"):
                    pe.wait_ge(normalised[int(task[1])], at.graph(ahead, 1, 1))
                elif task in ("v0", "q0", "k0"):
                    wait_out(pe, at, at.latest(s, "h0_turn", 1))
                    if at.first < 0 and part == 0:
                        pe.wait_ge({"q0": wq_loaded, "k0": wk_loaded, "v0": wv_loaded}[task], DMA)
                elif task == "out_proj":
                    wait_out(pe, at, at.latest(s, "pv", 1, "X"))
                    if at.first == 0 and part == 0:
                        pe.wait_ge(later_loaded, LATER_DMAS)
                elif task == "m":
                    wait_out(pe, at, at.latest(s, "h1_turn", 1))
                elif task == "m_turn":
                    wait_out(pe, at, at.latest(s, "m", 1))
                elif task in ("q1", "k1"):
                    wait_out(pe, at, at.latest(s, "m_turn", 1))
                elif task == "n_turn":
                    pe.wait_ge(n_ready, at.graph(ahead, 1, 1))
                elif task == "finish":
                    wait_out(pe, at, at.latest(s, "pv", 3, "Y"))
                elif task == "v1" and at.first == 0:
                    pe.wait_ge(bank_emptied["dve"], 2)

            def fill(at, n, s, piece, is_last):
                task, ahead, part = at.body.bank_tasks[n][1]
                if piece == 0:
                    dst = take_bank(at, n)
                    if task != "pv":
                        await_operands(at, s, task, ahead, part)
                dst = work_bank[at.bank_ring(n)]
                if task == "fold":
                    if part == 0:
                        for i in range(DC):
                            for c in range(DC):
                                col = i * dim + c * P
                                last = nc.tensor.matmul(dst[:, col:col + P], gcn_raw[:, c, i * P:(i + 1) * P],
                                                        head_blocks[:, :], start=True, stop=True)
                    else:
                        for c in range(DC):
                            last = nc.tensor.matmul(dst[:, c * P:(c + 1) * P], gcn_b_wide[:, c, :],
                                                    head_blocks[:, :], start=True, stop=True)
                elif task in ("h0_turn", "h1_turn"):
                    last = turn_tokens(dst, part)
                elif task == "v0":
                    last = project_tokens(dst, h_t, wv_sb, part, piece)
                elif task in ("q0", "k0"):
                    last = project_features(dst, wq_sb if task == "q0" else wk_sb, h_t, part, piece)
                elif task == "out_proj":
                    last = project_tokens(dst, o_t, wo_sb, part, piece)
                elif task == "m":
                    last = project_tokens(dst, h_t, map_sb, part, piece)
                elif task == "m_turn":
                    last = turn_tokens(dst, part)
                elif task in ("q1", "k1"):
                    last = project_features(dst, qw_sb if task == "q1" else kw_sb, m_t, part, piece)
                elif task == "n_turn":
                    last = turn_tokens(dst, part)
                elif task == "finish":
                    for t in range(2):
                        tile = (2 * part + t) * P
                        for c in range(DC):
                            col = t * dim + c * P
                            last = turn(dst[:, col:col + P], o_t[:, c, tile:tile + P])
                elif task == "v1":
                    last = project_tokens(dst, h_t, gcn_sb, part, piece)
                else:
                    last = times_values(at, s, dst, ahead, part, piece)
                if is_last:
                    last.then_inc(bank_filled, 1)

            def times_values(at, s, dst, kind, group, piece):
                n = at.body.lagged_number(s, LAG_PV)
                if piece == 0:
                    pe.wait_ge(turn_copied, at.units(n + 1))
                    if kind == "X":
                        wait_out(pe, at, at.latest(s, "v0", 1))
                    elif group == 0:
                        wait_out(pe, at, at.latest(s, "v1", 1))
                for c in range(piece * QT // 2, (piece + 1) * QT // 2):
                    if kind == "X":
                        for h in range(2):
                            col = (2 * group + h) * D0
                            r = at.unit_ring(n + 1 - GROUP + QT * h, TURN_RING)
                            last = nc.tensor.matmul(dst[D0 * h:D0 * h + D0, :], v0[:, c, col:col + D0],
                                                    prob_t[:, r:r + QT, c, :], start=c == 0, stop=c == QT - 1,
                                                    skip_group_check=True)
                    else:
                        for j in range(HC1):
                            col = ((group // 2) * HC1 + j) * D1
                            r = at.unit_ring(n + 1 - GROUP + 2 * j, TURN_RING)
                            last = nc.tensor.matmul(dst[D1 * j:D1 * j + D1, 0:HALF], v1[:, c, col:col + D1],
                                                    prob_t[:, r:r + 2, c, :], start=c == 0, stop=c == QT - 1,
                                                    skip_group_check=True)
                return last

            def scores(at, s, kind, u):
                n = at.body.unit_number(s)
                if at.n_units + n >= 2:
                    pe.wait_ge(masked, at.units(n - 1))
                dst = score_bank[at.unit_ring(n, 2)]
                if kind == "X":
                    head, _, t = unit_x(u)
                    if u == 0:
                        pe.wait_ge(q0_stacked, at.graph(1, STACK0_DMAS, STACK0_DMAS))
                        pe.wait_ge(k0_stacked, at.graph(1, STACK0_DMAS, STACK0_DMAS))
                    q = q0_stack[:, head, t * P:(t + 1) * P]
                    nc.tensor.matmul(dst[:, :], q, k0_high[:, head, :], start=True, stop=False)
                    nc.tensor.matmul(dst[:, :], q, k0_low[:, head, :], start=False, stop=True).then_inc(scores_ready, 1)
                else:
                    head, j, t, _ = unit_y(u)
                    if u < GROUP and u % 2 == 0:
                        pe.wait_ge(stacked[j], at.graph(-1, STACK1_DMAS, STACK1_DMAS))
                    nc.tensor.matmul(dst[:, :], q1_stack[:, head, t * P:(t + 1) * P], k1_stack[:, head, :],
                                     start=True, stop=True).then_inc(scores_ready, 1)

            def cosines(at, s, u):
                head, _, t, _ = unit_y(u)
                if u >= 2:
                    pe.wait_ge(picked, at.graph(graph_ahead(s, LAG_COS, "Y"), Y_SLOTS, u - 1))
                nc.tensor.matmul(cos_bank[u % 2][:, :], ns_stack[:, head, t * P:(t + 1) * P], nm_stack[:, head, :],
                                 start=True, stop=True).then_inc(cos_ready, 1)

            def turn_weights(at, s, kind, u):
                n = at.body.lagged_number(s, LAG_TURN)
                ahead = graph_ahead(s, LAG_TURN, kind)
                if kind == "X":
                    pe.wait_ge(normed, at.graph(ahead, X_SLOTS, u + 1))
                else:
                    pe.wait_ge(picked, at.graph(ahead, Y_SLOTS, u + 1))
                if at.n_units + n >= 2:
                    pe.wait_ge(turn_copied, at.units(n - 1))
                dst, r = turn_bank[at.unit_ring(n, 2)], at.unit_ring(n, 4)
                for c in range(QT):
                    last = turn(dst[:, c * P:(c + 1) * P], prob[:, r, c * P:(c + 1) * P])
                last.then_inc(turned, 1)

            pe.wait_ge(consts_made, 1)

            def emit(at):
                for s in range(N_SLOTS):
                    if at.body.units[s]:
                        scores(at, s, *at.body.units[s])
                    done = at.body.lagged(s, LAG_COS)
                    if done and done[0] == "Y":
                        cosines(at, s, done[1])
                    if at.body.lagged(s, LAG_TURN):
                        turn_weights(at, s, *at.body.lagged(s, LAG_TURN))
                    for n, start, piece, is_last in at.body.pieces[s]:
                        fill(at, n, start, piece, is_last)

            walk(pe, emit)

        @block.vector
        def _(dve):
            emptied = bank_emptied["dve"]

            def mask_and_max(at, s, kind, u):
                n = at.body.unit_number(s)
                dve.wait_ge(scores_ready, at.units(n + 1))
                if at.n_units + n >= 4:
                    dve.wait_ge(turned, at.units(n - 3))
                if kind == "X":
                    t, mask, scale = unit_x(u)[2], mask0, C0
                    if u == 0:
                        dve.wait_ge(masks_made, mask_number(at, 0))
                else:
                    t, mask, scale = unit_y(u)[2], mask1, C1
                    if u == 0:
                        dve.wait_ge(masks_made, at.graph(0, 2, 1 if at.first < graphs else 0))
                wait_apart(dve)
                r = at.unit_ring(n, 4)
                nc.vector.tensor_tensor_reduce(out=prob[:, r, :], in0=score_bank[at.unit_ring(n, 2)][:, :],
                                               in1=mask[:, t, :], scale=-scale, scalar=BIG, op0=ALU.add, op1=ALU.min,
                                               accum_out=row_min[:, r:r + 1]).then_inc(masked, 1)

            def select(at, s, kind, u):
                n = at.body.lagged_number(s, LAG_SELECT)
                dve.wait_ge(exped, at.units(n + 1))
                r = at.unit_ring(n, 4)
                if kind == "X":
                    nc.vector.reciprocal(inv0[:, u:u + 1], sum0[:, u:u + 1]).then_inc(inverted, 1)
                else:
                    head, _, t, _ = unit_y(u)
                    dve.wait_ge(cos_ready, at.graph(graph_ahead(s, LAG_SELECT, kind), Y_SLOTS, u + 1))
                    nc.vector.scalar_tensor_tensor(out=prob[:, r, :], in0=cos_bank[u % 2][:, :], scalar=COS_MIN,
                                                   in1=prob[:, r, :], op0=ALU.is_gt, op1=ALU.mult,
                                                   accum_out=picked1[:, t, head:head + 1]).then_inc(picked, 1)

            def row_stats(at, ahead, layer, src):
                for t in range(QT):
                    last = nc.vector.bn_stats(stats[:, t, :], src[:, t, :])
                last.then_inc(stats_taken[layer], 1)
                dve.wait_ge(stats_taken[layer], at.graph(ahead, 1, 1))
                if at.first + ahead >= 1:
                    dve.wait_ge(normalised[layer], at.graph(ahead, 1, 0))
                wait_apart(dve)
                for t in range(QT):
                    last = nc.vector.bn_aggr(mean_var[layer][:, t, :], stats[:, t, :])
                last.then_inc(stats_ready[layer], 1)

            def row_factors(at, ahead):
                dve.wait_ge(picked, at.graph(ahead, Y_SLOTS, Y_SLOTS))
                nc.vector.tensor_tensor(factor[:, :, :], sum1[:, :, :], picked1[:, :, :], ALU.add).then_inc(factor_step, 1)
                nc.vector.tensor_scalar(keep_row[:, :], mask1[:, :, 0], NEG1 / 2, None, ALU.is_gt).then_inc(factor_step, 1)
                dve.wait_ge(factor_step, at.graph(ahead, 3, 2))
                nc.vector.reciprocal(factor[:, :, :], factor[:, :, :]).then_inc(factor_step, 1)
                dve.wait_ge(factor_step, at.graph(ahead, 3, 3))
                nc.vector.tensor_tensor(factor[:, :, :], factor[:, :, :],
                                        keep_row[:, :].unsqueeze(2).broadcast_to([P, QT, H1]),
                                        ALU.mult).then_inc(factors_ready, 1)

            def empty(at, n, s, task, ahead, part):
                dve.wait_ge(bank_filled, at.banks(n + 1))
                src = work_bank[at.bank_ring(n)]
                src_tiles = src[:, :].rearrange("p (t d) -> p t d", t=2)
                pair = slice(2 * part, 2 * part + 2)
                if task == "fold":
                    if part == 0:
                        nc.vector.tensor_copy(gcn_sb[:, :, :], src_tiles).then_inc(emptied, 1)
                    else:
                        nc.vector.tensor_copy(gcn_b_row[:, :], src[:, 0:dim]).then_inc(emptied, 1)
                elif task == "out_proj":
                    dve.wait_ge(bo_added, at.graph(ahead, 1, 1))
                    nc.vector.tensor_tensor(x_now[:, pair, :], src_tiles, x_now[:, pair, :], ALU.add).then_inc(emptied, 1)
                elif task in ("m", "v1"):
                    if at.first == 0 and task == "v1":
                        dve.wait_ge(emptied, 2)
                    dst, bias = (tok, map_b_row) if task == "m" else (v1, gcn_b_row)
                    nc.vector.tensor_tensor(dst[:, pair, :], src_tiles,
                                            bias[:, :].unsqueeze(1).broadcast_to([P, 2, dim]), ALU.add).then_inc(emptied, 1)
                elif task == "finish":
                    dve.wait_ge(factors_ready, at.graph(ahead, 1, 1))
                    heads = factor[:, pair, :].rearrange("p t h -> p (t h)").unsqueeze(2).broadcast_to([P, 2 * H1, D1])
                    src_heads = src[:, :].rearrange("p (h d) -> p h d", d=D1)
                    nc.vector.tensor_tensor(src_heads, src_heads, heads, ALU.mult).then_inc(scaled, 1)
                    dve.wait_ge(scaled, at.graph(ahead, 2, part + 1))
                    dve.wait_ge(x1_copied, at.graph(ahead, 1, 1))
                    nc.vector.scalar_tensor_tensor(out=x1_kept[:, pair, :], in0=src_tiles, scalar=0.0,
                                                   in1=x1_kept[:, pair, :], op0=ALU.max, op1=ALU.add).then_inc(emptied, 1)
                else:
                    dst, bias = {"q0": (q_parts, None), "k0": (k_parts, None), "n_turn": (n_parts, None),
                                 "q1": (q_parts, q_b_col), "k1": (k_parts, k_b_col)}[task]
                    high, low = dst[:, part, 0, :], dst[:, part, 1, :].bitcast(F32R)
                    dve.wait_ge(high_ready[task], at.graph(ahead, DC, part + 1))
                    if bias is None:
                        nc.vector.tensor_tensor(low, src[:, :], high, ALU.subtract).then_inc(emptied, 1)
                    else:
                        nc.vector.scalar_tensor_tensor(out=low, in0=src[:, :], scalar=bias[:, part:part + 1], in1=high,
                                                       op0=ALU.add, op1=ALU.subtract).then_inc(emptied, 1)

            def step(at, s, task, ahead):
                if task == "ln0_stats":
                    dve.wait_ge(tok_loaded, at.graph(ahead, DMA, DMA))
                    row_stats(at, ahead, 0, tok)
                elif task == "ln1_stats":
                    wait_out(dve, at, at.latest(s, "out_proj", 1))
                    row_stats(at, ahead, 1, x_now)
                elif task == "m_sums":
                    dve.wait_ge(squared, at.graph(ahead, 2, 2))
                    if at.first + ahead >= 1:
                        dve.wait_ge(inv_norm_ready, at.graph(ahead, 1, 0))
                    squares = m_t[:, :, :].rearrange("p c n -> p (c n)").rearrange("p (a d) -> p a d", d=D1)
                    nc.vector.reduce_sum(norm2[:, :], squares, AX_X).then_inc(summed, 1)
                elif task == "row_factors":
                    row_factors(at, ahead)
                elif task == "keep_x1":
                    if at.first >= 1:
                        dve.wait_ge(y_stored, at.graph(-1, DMA, DMA))
                    nc.vector.tensor_copy(x1_kept[:, :, :], x_now[:, :, :]).then_inc(x1_copied, 1)

            dve.wait_ge(fold_loaded, FOLD_DMAS)
            nc.vector.tensor_copy(gcn_b_wide[:, :, :],
                                  gcn_b_col[:, :].unsqueeze(2).broadcast_to([P, DC, P])).then_inc(bias_widened, 1)

            def emit(at):
                for s in range(N_SLOTS):
                    for n in at.body.emptying[s]:
                        task, ahead, part = at.body.bank_tasks[n][1]
                        if PSUM_TASKS[task] == "dve":
                            empty(at, n, s, task, ahead, part)
                    if at.body.units[s]:
                        mask_and_max(at, s, *at.body.units[s])
                    if at.body.lagged(s, LAG_SELECT):
                        select(at, s, *at.body.lagged(s, LAG_SELECT))
                    for task, ahead, _ in at.body.tasks[s]:
                        if task not in PSUM_TASKS:
                            step(at, s, task, ahead)

            walk(dve, emit)

        @block.scalar
        def _(act):
            emptied = bank_emptied["act"]

            def exp(at, s, kind, u):
                n = at.body.unit_number(s)
                act.wait_ge(masked, at.units(n + 1))
                r = at.unit_ring(n, 4)
                if kind == "X":
                    total = sum0[:, u:u + 1]
                else:
                    head, _, t, _ = unit_y(u)
                    total = sum1[:, t, head:head + 1]
                nc.scalar.activation(prob[:, r, :], prob[:, r, :], ACT.Exp, bias=row_min[:, r:r + 1], scale=-1.0,
                                     accum_out=total).then_inc(exped, 1)

            def copy_turned(at, s, kind, u):
                n = at.body.lagged_number(s, LAG_TURN)
                act.wait_ge(turned, at.units(n + 1))
                if u % GROUP == TURN_RING - GROUP and at.n_units + n >= GROUP:
                    act.wait_ge(bank_filled, at.banks(at.latest(s, "pv") + 1))
                nc.scalar.copy(prob_t[:, at.unit_ring(n, TURN_RING)].rearrange("p c q -> p (c q)"),
                               turn_bank[at.unit_ring(n, 2)][:, :]).then_inc(turn_copied, 1)

            def empty(at, n, s, task, ahead, part):
                if task in ("fold", "out_proj", "m", "v1", "finish"):
                    return
                act.wait_ge(bank_filled, at.banks(n + 1))
                src = work_bank[at.bank_ring(n)]
                if task == "pv":
                    if ahead == "X":
                        nc.scalar.copy(o_t[:, part, :], src[:, :]).then_inc(emptied, 1)
                    else:
                        half = (part % 2) * HALF
                        nc.scalar.copy(o_t[:, part // 2, half:half + HALF], src[:, 0:HALF]).then_inc(emptied, 1)
                elif task in ("h0_turn", "h1_turn"):
                    nc.scalar.activation(h_t[:, part, :], src[:, :], ACT.Relu).then_inc(emptied, 1)
                elif task == "v0":
                    nc.scalar.copy(v0[:, 2 * part:2 * part + 2, :],
                                   src[:, :].rearrange("p (t d) -> p t d", t=2)).then_inc(emptied, 1)
                elif task == "m_turn":
                    if part == 0:
                        act.wait_ge(summed, at.graph(ahead, 1, 1))
                    nc.scalar.copy(m_t[:, part, :], src[:, :]).then_inc(emptied, 1)
                else:
                    if part == 0 and task in ("q0", "k0", "n_turn") and at.first >= 1:
                        for j in range(HC1):
                            act.wait_ge(stacked[j], at.graph(0, STACK1_DMAS, 0))
                    if part == 0 and task in ("q1", "k1"):
                        latest = 1 if at.first + 1 < graphs else 0
                        if task == "q1":
                            act.wait_ge(q0_stacked, at.graph(latest, STACK0_DMAS, STACK0_DMAS))
                        else:
                            act.wait_ge(k0_stacked, at.graph(latest, STACK0_DMAS, STACK0_DMAS))
                    dst, bias = {"q0": (q_parts, None), "k0": (k_parts, None), "n_turn": (n_parts, None),
                                 "q1": (q_parts, q_b_col), "k1": (k_parts, k_b_col)}[task]
                    high = dst[:, part, 0, :].bitcast(F32R)
                    if bias is None:
                        nc.scalar.activation(high, src[:, :], ACT.Identity).then_inc(high_ready[task], 1)
                    else:
                        nc.scalar.activation(high, src[:, :], ACT.Identity,
                                             bias=bias[:, part:part + 1]).then_inc(high_ready[task], 1)

            def emit(at):
                for s in range(N_SLOTS):
                    for n in at.body.emptying[s]:
                        empty(at, n, s, *at.body.bank_tasks[n][1])
                    if at.body.lagged(s, LAG_TURN):
                        copy_turned(at, s, *at.body.lagged(s, LAG_TURN))
                    if at.body.units[s]:
                        exp(at, s, *at.body.units[s])
                    for task, ahead, part in at.body.tasks[s]:
                        if task == "m_square":
                            wait_out(act, at, at.latest(s, "m", part))
                            pair = slice(part * HALF * dim // P, (part + 1) * HALF * dim // P)
                            nc.scalar.activation(m_t[:, :, :].rearrange("p c n -> p (c n)")[:, pair],
                                                 tok[:, :, :].rearrange("p t d -> p (t d)")[:, pair],
                                                 ACT.Square).then_inc(squared, 1)

            walk(act, emit)

        @block.gpsimd
        def _(pool):
            def normalise(at, ahead, layer, src):
                pool.wait_ge(stats_ready[layer], at.graph(ahead, 1, 1))
                wait_apart(pool)
                nc.gpsimd.tensor_scalar(minus_mean[:, :], mean_var[layer][:, :, 0], -1.0, 0.0,
                                        ALU.mult, ALU.add).then_inc(norm_step[layer], 1)
                nc.gpsimd.tensor_scalar(var_eps[:, :], mean_var[layer][:, :, 1], LN_EPS, 1.0,
                                        ALU.add, ALU.mult).then_inc(norm_step[layer], 1)
                pool.wait_ge(norm_step[layer], at.graph(ahead, 3, 2))
                nc.gpsimd.tensor_tensor(rstd[:, :], var_eps[:, :], minus_half[:, 0:QT], ALU.pow).then_inc(norm_step[layer], 1)
                pool.wait_ge(norm_step[layer], at.graph(ahead, 3, 3))
                wait_apart(pool)
                for t in range(QT):
                    last = nc.gpsimd.tensor_scalar(tok[:, t, :], src[:, t, :], minus_mean[:, t:t + 1], rstd[:, t:t + 1],
                                                   ALU.add, ALU.mult)
                last.then_inc(normalised[layer], 1)

            def make_mask(at, layer):
                number = mask_number(at, layer)
                pool.wait_ge(adj_loaded, number * DMA)
                if layer == 0:
                    if at.body.before is not None:
                        pool.wait_ge(masked, at.units(0))
                    wait_apart(pool)
                    nc.gpsimd.tensor_scalar(mask0[:, :, :], adj_raw[:, :, :], -1.0, -NEG0,
                                            ALU.add, ALU.mult).then_inc(masks_made, 1)
                else:
                    if at.first >= 1:
                        pool.wait_ge(factors_ready, at.graph(0, 1, 0))
                    wait_apart(pool)
                    nc.gpsimd.tensor_scalar(mask1[:, :, :], adj_raw[:, :, :], NEG1, 0.0,
                                            ALU.mult, ALU.add).then_inc(masks_made, 1)

            def step(at, s, task, ahead):
                if task == "ln0_apply":
                    normalise(at, ahead, 0, tok)
                elif task == "ln1_apply":
                    wait_out(pool, at, at.latest(s, "h0_turn" if at.first + 1 < graphs else "n_turn", 1))
                    normalise(at, ahead, 1, x_now)
                elif task == "add_bo":
                    pool.wait_ge(x_loaded, at.graph(ahead, DMA, DMA))
                    if at.first == 0:
                        pool.wait_ge(later_loaded, LATER_DMAS)
                    nc.gpsimd.tensor_tensor(x_now[:, :, :], x_now[:, :, :],
                                            bo_row[:, :].unsqueeze(1).broadcast_to([P, QT, dim]),
                                            ALU.add).then_inc(bo_added, 1)
                elif task in ("mask0", "mask1"):
                    make_mask(at, int(task[-1]))
                elif task == "m_norms":
                    pool.wait_ge(summed, at.graph(ahead, 1, 1))
                    wait_apart(pool)
                    nc.gpsimd.tensor_scalar(floored[:, :], norm2[:, :], NORM_FLOOR, BIG,
                                            ALU.max, ALU.min).then_inc(norms_floored, 1)
                    pool.wait_ge(norms_floored, at.graph(ahead, 1, 1))
                    nc.gpsimd.tensor_tensor(inv_norm[:, :], floored[:, :], minus_half[:, :], ALU.pow).then_inc(inv_norm_ready, 1)
                elif task == "n_scale":
                    wait_out(pool, at, at.latest(s, "m_turn", 1))
                    pool.wait_ge(inv_norm_ready, at.graph(ahead, 1, 1))
                    heads = tok[:, :, :].rearrange("p t d -> p (t d)").rearrange("p (a d) -> p a d", d=D1)
                    nc.gpsimd.tensor_tensor(heads, heads, inv_norm[:, :].unsqueeze(2).broadcast_to([P, QT * H1, D1]),
                                            ALU.mult).then_inc(n_ready, 1)

            nc.gpsimd.memset(head_blocks[:, :], 0.0).then_inc(blocks_zeroed, 1)
            nc.gpsimd.memset(minus_half[:, :], -0.5)
            nc.gpsimd.memset(ident[:, :], 0.0).then_inc(ident_zeroed, 1)
            pool.wait_ge(ident_zeroed, 1)
            nc.gpsimd.affine_select(out=ident[:, :], in_=ident[:, :], compare_op=ALU.not_equal, fill=1.0, base=0,
                                    pattern=[[-1, P]], channel_multiplier=1).then_inc(consts_made, 1)
            pool.wait_ge(consts_made, 1)

            def emit(at):
                for s in range(N_SLOTS):
                    done = at.body.lagged(s, LAG_SELECT)
                    if done and done[0] == "X":
                        u, r = done[1], at.unit_ring(at.body.lagged_number(s, LAG_SELECT), 4)
                        pool.wait_ge(inverted, at.graph(graph_ahead(s, LAG_SELECT, "X"), X_SLOTS, u + 1))
                        wait_apart(pool)
                        nc.gpsimd.tensor_scalar(prob[:, r, :], prob[:, r, :], inv0[:, u:u + 1], 1.0,
                                                ALU.mult, ALU.mult).then_inc(normed, 1)
                    for task, ahead, _ in at.body.tasks[s]:
                        if task not in PSUM_TASKS:
                            step(at, s, task, ahead)

            walk(pool, emit)


_OUT_SHAPE = (16, 512, 256)


def kernel(**inputs):
    import numpy as np
    import concourse.bacc as bacc
    from concourse.bass_utils import run_bass_kernel_spmd

    def laid(name, turned=False):
        a = np.asarray(inputs[name])
        return np.ascontiguousarray(a.T if turned else a)

    def column(name):
        return np.ascontiguousarray(np.asarray(inputs[name]).reshape(-1, P).T)

    arrays = {
        "x": laid("x"), "adj": laid("adj"),
        "wq": laid("L0_gnn_Wq"), "wk": laid("L0_gnn_Wk"), "wv": laid("L0_gnn_Wv"), "wo": laid("L0_gnn_Wo"),
        "bo": laid("L0_gnn_bo"),
        "map_w": laid("L1_gnn_map_w", True), "map_b": laid("L1_gnn_map_b"),
        "q_w": laid("L1_gnn_q_w", True), "q_b": column("L1_gnn_q_b"),
        "k_w": laid("L1_gnn_k_w", True), "k_b": column("L1_gnn_k_b"),
        "gcn_w": laid("L1_gnn_gcn_map_w"), "gcn_b": column("L1_gnn_gcn_map_b"),
        "gcn_head_w": laid("L1_gnn_gcn_W", True),
    }
    nc = bacc.Bacc("TRN2", target_bir_lowering=False, num_devices=1)
    args = [nc.dram_tensor(f"{n}_dram", a.shape, mybir.dt.from_np(a.dtype), kind="ExternalInput").ap()
            for n, a in arrays.items()]
    out = nc.dram_tensor("out_dram", _OUT_SHAPE, F32, kind="ExternalOutput").ap()
    attention_layers(nc, *args, out)
    r = run_bass_kernel_spmd(nc, [{f"{n}_dram": a for n, a in arrays.items()}], core_ids=[0])
    return r.results[0]["out_dram"]
```

```python
from contextlib import ExitStack

import concourse.bass as bass
from concourse import mybir

F32 = mybir.dt.float32
F32R = mybir.dt.float32r
BF16 = mybir.dt.bfloat16
U8 = mybir.dt.uint8
ALU = mybir.AluOpType
ACT = mybir.ActivationFunctionType
AX_X = mybir.AxisListType.X

P = 128
BANK = 512
NEG0 = -3.3895e38
NEG1 = -1e10
LN_EPS = 1e-5
NORM_FLOOR = 1e-16
COS_MIN = 0.1
BIG = 3.4e38

Y_SLOTS, X_SLOTS = 32, 16
N_SLOTS = Y_SLOTS + X_SLOTS
GROUP = 8
PROB_RING = 6
TURN_RING = 12
WORK_BANKS = 3
LAG_COS, LAG_SELECT, LAG_TURN, LAG_PV = 1, 1, 4, 5

SLOTS = {
    0: [("v0", 1, 0)], 2: [("add_bo", 0, 0)], 5: [("q0", 1, 0)], 7: [("out_proj", 0, 0)], 8: [("ln1_apply", 0, 0)],
    9: [("out_proj", 0, 1), ("ln1_stats", 0, 0), ("ln1_apply", 0, 1), ("ln1_apply", 0, 2), ("ln1_apply", 0, 3)],
    10: [("k0", 1, 0)], 11: [("ln1_stats", 0, 1), ("q0", 1, 1)], 13: [("k0", 1, 1)], 14: [("mask0", 1, 0)],
    15: [("h1_turn", 0, 0)], 16: [("h1_turn", 0, 1), ("v0", 1, 1)], 18: [("mv", 0, 0), ("keep_v0", 1, 0)],
    19: [("mv", 0, 1)], 20: [("m_norms", 0, 0)], 21: [("m_square", 0, 0), ("mv", 0, 2), ("m_square", 0, 1)],
    22: [("mv", 0, 3), ("m_sums", 0, 0)], 23: [("q1", 0, 0)], 24: [("q1", 0, 1), ("m_square", 0, 2)],
    25: [("k1", 0, 0), ("m_square", 0, 3), ("m_sums", 0, 1),
        ("n_scale", 0, 0), ("m_norms", 0, 1), ("n_scale", 0, 1)],
    26: [("k1", 0, 1)], 31: [("n_turn", 0, 0)], 32: [("n_turn", 0, 1)],
    36: [("row_factors", -1, 0), ("ln0_stats", 2, 0)],
    37: [("ln0_stats", 2, 1), ("ln0_apply", 2, 0), ("ln0_apply", 2, 1)], 38: [("finish", -1, 0)],
    39: [("finish", -1, 1), ("mask1", 0, 0)], 40: [("mask1", 0, 1), ("ln0_apply", 2, 2), ("ln0_apply", 2, 3)],
    41: [("mask1", 0, 2), ("keep_v1", 0, 0)], 42: [("mask1", 0, 3)], 43: [("h0_turn", 2, 0), ("h0_turn", 2, 1)],
    44: [("keep_x1", 0, 0), ("keep_v1", 0, 1)],
}
FIRST_SLOTS = {
    0: [("ln0_stats", 1, 0), ("ln0_stats", 1, 1), ("ln0_apply", 1, 0), ("ln0_apply", 1, 1), ("ln0_apply", 1, 2),
        ("ln0_apply", 1, 3), ("h0_turn", 1, 0), ("h0_turn", 1, 1),
        ("split", 1, 0), ("split", 1, 1)],
    18: [("split", 1, 2)],
    19: [("fold", 1, 0)], 20: [("fold", 1, 1)], 21: [("fold", 1, 2)], 22: [("fold", 1, 3)], 23: [("fold", 1, 4)],
}
FOLD_GCN, FOLD_GCN_B, FOLD_Q, FOLD_K, FOLD_QK_B = range(5)
PSUM_TASKS = {"h0_turn": "dve", "v0": "act", "out_proj": "dve", "q0": "dve", "k0": "dve",
              "h1_turn": "dve", "mv": "dve", "q1": "dve", "k1": "dve",
              "n_turn": "dve", "finish": "dve", "fold": "dve", "pv": "act"}
TWO_PIECES = ("v0", "out_proj", "q0", "k0", "mv", "q1", "k1", "pv")


class Body:

    def __init__(self, k, graphs, before):
        self.units = [None] * N_SLOTS
        if k >= 1:
            self.units[:Y_SLOTS] = [("Y", u) for u in range(Y_SLOTS)]
        if k + 1 < graphs:
            self.units[Y_SLOTS:] = [("X", u) for u in range(X_SLOTS)]
        self.before = before
        self.tasks = []
        self.last = 0
        for s in range(N_SLOTS):
            here = list(FIRST_SLOTS.get(s, [])) if k == -1 else []
            for task, ahead, part in SLOTS.get(s, []):
                if 0 <= k + ahead < graphs:
                    here.append((task, ahead, part))
            done = self.lagged(s, LAG_PV)
            if done and done[1] % GROUP == GROUP - 1:
                here.append(("pv", done[0], done[1] // GROUP))
            self.tasks.append(here)
        self.bank_tasks = [(s, t) for s, here in enumerate(self.tasks) for t in here if t[0] in PSUM_TASKS]
        self.pieces = [[] for _ in range(N_SLOTS)]
        self.emptying = [[] for _ in range(N_SLOTS)]
        for n, (s, t) in enumerate(self.bank_tasks):
            count = 2 if t[0] in TWO_PIECES else 1
            for piece in range(count):
                self.pieces[s + piece].append((n, s, piece, piece == count - 1))
            self.emptying[s + count].append(n)
        ended = [n for s in range(N_SLOTS) for n, _, _, last in self.pieces[s] if last]
        assert ended == sorted(ended)
        self.n_units = sum(u is not None for u in self.units)

    def lagged(self, s, lag):
        if s >= lag:
            return self.units[s - lag]
        return self.before.units[N_SLOTS + s - lag] if self.before else None

    def unit_number(self, s):
        return sum(u is not None for u in self.units[:s])

    def lagged_number(self, s, lag):
        if s >= lag:
            return self.unit_number(s - lag)
        return self.before.unit_number(N_SLOTS + s - lag) - self.before.n_units

    def emptied(self, engine):
        return sum(PSUM_TASKS[t[0]] == engine for _, t in self.bank_tasks)


class At:

    def __init__(self, k, body, units, banks, emptied, first=None, step=None):
        self.k, self.body = k, body
        self.first = k if first is None else first
        self.n_units, self.n_banks, self.n_emptied, self.step = units, banks, emptied, step

    def _passes(self, value, per_pass):
        return value if self.step is None else (self.k - self.first) * per_pass + value

    def units(self, n):
        return self._passes(self.n_units + n, self.step and self.step[0])

    def unit_ring(self, n, size):
        return (self.n_units + n) % size

    def banks(self, n):
        return self._passes(self.n_banks + n, self.step and self.step[1])

    def bank_ring(self, n):
        return (self.n_banks + n) % WORK_BANKS

    def _emptied(self, engine, n):
        return self._passes(self.n_emptied[engine] + n, self.step and self.step[2][engine])

    def emptied(self, i):
        tasks = self.body.bank_tasks if i >= 0 else self.body.before.bank_tasks
        engine = PSUM_TASKS[tasks[i][1][0]]
        if i >= 0:
            return engine, self._emptied(engine, sum(PSUM_TASKS[t[0]] == engine for _, t in tasks[:i + 1]))
        return engine, self._emptied(engine, 1 - sum(PSUM_TASKS[t[0]] == engine for _, t in tasks[i:]))

    def latest(self, s, task, part=None, which=None):
        def found(tasks, until):
            return [i for i, (at, t) in enumerate(tasks)
                    if at <= until and t[0] == task and part in (None, t[2]) and which in (None, t[1])]
        here = found(self.body.bank_tasks, s)
        if here:
            return here[-1]
        before = self.body.before.bank_tasks
        return found(before, N_SLOTS)[-1] - len(before)

    def graph(self, ahead, each, plus):
        return (self.k + ahead) * each + plus


def attention_layers(nc, x, adj, wq, wk, wv, wo, bo, map_w, map_rows, map_b, map_b_cols,
                     qk_b, q_w, k_w, gcn_w, gcn_b, gcn_head_w, out):
    graphs, tokens, dim = x.shape
    QT = tokens // P
    DC = dim // P
    H0, H1 = 4, 8
    D0, D1 = dim // H0, dim // H1
    HC0, HC1 = H0 // DC, H1 // DC
    HALF = tokens // 2
    C0, C1 = float(D0) ** -0.5, float(D1) ** -0.5
    DMA = 16
    LATER_DMAS = (6 + 4 + 2 + HC1) * DMA
    Q0_DMAS, K0_DMAS = 2 * HC0 * DMA, 4 * HC0 * DMA
    STACK1_DMAS = 2 * HC1 * DMA
    assert (QT, DC, D0, D1, tokens) == (4, 2, 64, 32, BANK)

    body_first = Body(-1, graphs, None)
    body_0 = Body(0, graphs, body_first)
    body_loop = Body(1, graphs, body_0)
    body_14 = Body(graphs - 2, graphs, body_loop)
    body_15 = Body(graphs - 1, graphs, body_14)
    body_16 = Body(graphs, graphs, body_15)
    LOOP_FROM, LOOP_TO = 1, graphs - 2
    ats, units, banks, emptied = {}, 0, 0, {"act": 0, "dve": 0}
    for name, k, body, passes in (("first", -1, body_first, 1), ("0", 0, body_0, 1),
                                  ("loop", 1, body_loop, LOOP_TO - LOOP_FROM),
                                  ("14", graphs - 2, body_14, 1), ("15", graphs - 1, body_15, 1),
                                  ("16", graphs, body_16, 1)):
        ats[name] = (k, body, units, banks, dict(emptied))
        units += passes * body.n_units
        banks += passes * len(body.bank_tasks)
        for e in emptied:
            emptied[e] += passes * body.emptied(e)
    loop_step = (body_loop.n_units, len(body_loop.bank_tasks), {e: body_loop.emptied(e) for e in emptied})
    assert loop_step[0] % PROB_RING == loop_step[0] % TURN_RING == 0 and loop_step[1] % WORK_BANKS == 0
    ended = [t[0] for _, t in body_loop.bank_tasks[::-1]].index("finish")
    assert ended >= WORK_BANKS and body_0.bank_tasks[-ended:] == body_loop.bank_tasks[-ended:]

    def walk(engine, emit):
        for name in ("first", "0"):
            emit(At(*ats[name]))
        with engine.Fori(LOOP_FROM, LOOP_TO) as k:
            emit(At(k, *ats["loop"][1:], first=LOOP_FROM, step=loop_step))
        for name in ("14", "15", "16"):
            emit(At(*ats[name]))

    ctx = ExitStack()
    with ctx:
        def sb(name, shape, dt=F32):
            return ctx.enter_context(nc.sbuf_tensor(name, shape, dt))

        def sem(name):
            return ctx.enter_context(nc.semaphore(name))

        wv_sb, wo_sb = sb("wv_sb", [P, DC, dim]), sb("wo_sb", [P, DC, dim])
        q0_w, k0_w, q1_w, k1_w = (sb(n, [P, 2, DC, dim], F32R) for n in ("q0_w", "k0_w", "q1_w", "k1_w"))
        mv_w = sb("mv_w", [P, 2, DC, 2, dim], F32R)
        gcn_b_col, map_b_col = sb("gcn_b_col", [P, DC]), sb("map_b_col", [P, DC])
        bo_row, mv_bias = sb("bo_row", [P, dim]), sb("mv_bias", [P, 2, dim])
        qk_b_raw, qk_b_cols = sb("qk_b_raw", [P, 2 * DC]), sb("qk_b_cols", [P, 2 * DC])
        q_b_col, k_b_col = qk_b_cols[:, 0:DC], qk_b_cols[:, DC:2 * DC]
        ident = sb("ident", [P, P])
        minus_half = sb("minus_half", [P, QT * H1])
        stationary_stacks = sb("stationary_stacks", [P, 2, H1, tokens], F32R)
        q1_stack, ns_stack = stationary_stacks[:, 0], stationary_stacks[:, 1]
        moving_stacks = sb("moving_stacks", [P, 2, H1, tokens], F32R)
        nm_stack, k1_stack = moving_stacks[:, 0], moving_stacks[:, 1]
        q0_stack = stationary_stacks[:, 0, 0:H0]
        k0_high, k0_low = moving_stacks[:, 0, 0:H0], moving_stacks[:, 1, 0:H0]
        parts = sb("parts", [P, 3, DC, 2, tokens])
        q_parts, n_parts, k_parts = parts[:, 0], parts[:, 1], parts[:, 2]
        h_whole = sb("h_whole", [P, DC, tokens])
        h_high, h_low = sb("h_high", [P, DC, tokens], F32R), sb("h_low", [P, DC, tokens], F32R)
        tok_v = sb("tok_v", [P, 2, QT, dim])
        tok = tok_v[:, 0]
        v_next = tok_v[:, 1]
        squares = parts[:, 1].rearrange("p c w n -> p (c w n)")[:, 0:QT * dim]
        v0, v1 = sb("v0_sb", [P, QT, dim]), sb("v1_sb", [P, QT, dim])
        x_now = sb("x_now", [P, QT, dim])
        x1_kept = sb("x1_kept", [P, QT, dim])
        head_blocks = x1_kept[:, 0, 0:P]
        gcn_b_wide = x1_kept[:, 1].rearrange("p (c q) -> p c q", c=DC)
        o_t = sb("o_t", [P, DC, tokens])
        adj_raw = sb("adj_raw", [P, QT, tokens], U8)
        mask0, mask1 = sb("mask0_sb", [P, QT, tokens], BF16), sb("mask1_sb", [P, QT, tokens], BF16)
        prob = sb("prob", [P, PROB_RING, tokens])
        prob_t = sb("prob_t", [P, TURN_RING, QT, P])
        wq_raw, wk_raw, map_raw, gcn_raw, map_rows_raw, qw_raw, kw_raw = (
            prob_t[:, i].rearrange("p c q -> p (c q)").rearrange("p (c n) -> p c n", c=DC) for i in range(7))
        row_min = sb("row_min", [P, PROB_RING])
        sum0, inv0 = sb("sum0", [P, X_SLOTS]), sb("inv0", [P, X_SLOTS])
        sum1, picked1 = sb("sum1", [P, QT, H1]), sb("picked1", [P, QT, H1])
        factor, keep_row = sb("factor", [P, QT, H1]), sb("keep_row", [P, QT])
        stats = sb("stats", [P, QT, 6])
        mean_var = [sb("mean_var0", [P, QT, 2]), sb("mean_var1", [P, QT, 2])]
        minus_mean, var_eps, rstd = sb("minus_mean", [P, QT]), sb("var_eps", [P, QT]), sb("rstd", [P, QT])
        norm2, floored, inv_norm = (sb(n, [P, QT * H1]) for n in ("norm2", "floored", "inv_norm"))

        def bank(name):
            return ctx.enter_context(nc.psum_tensor(name, [P, BANK], F32))

        score_bank = [bank("score0"), bank("score1")]
        cos_bank = bank("cos")
        turn_bank = [bank("turn0"), bank("turn1")]
        work_bank = [bank(f"work{i}") for i in range(WORK_BANKS)]

        blocks_zeroed = sem("blocks_zeroed")
        wq_loaded, wk_loaded, wv_loaded = sem("wq_loaded"), sem("wk_loaded"), sem("wv_loaded")
        later_loaded = sem("later_loaded")
        split_high, split_low = sem("split_high"), sem("split_low")
        ident_zeroed, consts_made, bias_widened = sem("ident_zeroed"), sem("consts_made"), sem("bias_widened")
        waits_passed = sem("waits_passed")
        scores_ready, masked, exped, turned, turn_copied = (
            sem(n) for n in ("scores_ready", "masked", "exped", "turned", "turn_copied"))
        inverted, normed = sem("inverted"), sem("normed")
        cos_ready, picked = sem("cos_ready"), sem("picked")
        bank_filled = sem("bank_filled")
        bank_emptied = {"act": sem("bank_emptied_act"), "dve": sem("bank_emptied_dve")}
        tok_loaded, x_loaded, adj_loaded, y_stored = (
            sem(n) for n in ("tok_loaded", "x_loaded", "adj_loaded", "y_stored"))
        stats_taken = [sem("stats0_taken"), sem("stats1_taken")]
        stats_ready = [sem("stats0_ready"), sem("stats1_ready")]
        norm_step = [sem("norm0_step"), sem("norm1_step")]
        normalised = [sem("normalised0"), sem("normalised1")]
        high_ready = {n: sem(n + "_high_ready") for n in ("q0", "k0", "q1", "k1", "n_turn", "h0_turn", "h1_turn", "fold")}
        q0_stacked, k0_stacked = sem("q0_stacked"), sem("k0_stacked")
        stacked = [sem(f"stacked{j}") for j in range(HC1)]
        v0_kept, v1_kept = sem("v0_kept"), sem("v1_kept")
        bo_added, x1_copied = sem("bo_added"), sem("x1_copied")
        masks_made = sem("masks_made")
        squared, summed, norms_floored, inv_norm_ready, n_ready = (
            sem(n) for n in ("squared", "summed", "norms_floored", "inv_norm_ready", "n_ready"))
        factor_step, factors_ready, scaled = sem("factor_step"), sem("factors_ready"), sem("scaled")

        def unit_x(u):
            pair, rest = divmod(u, GROUP)
            h, t = divmod(rest, QT)
            return pair * 2 + h, h, t

        def unit_y(u):
            group, rest = divmod(u, GROUP)
            j, q2 = divmod(rest, 2)
            return (group // 2) * HC1 + j, j, (group % 2) * 2 + q2, q2

        def graph_ahead(s, lag, kind):
            return {"X": 1, "Y": -1}[kind] - (1 if s < lag else 0)

        def mask_number(at, layer):
            if at.first < 0:
                return 1
            return at.graph(0, 2, 2 + (layer if at.first + 1 < graphs else 0))

        def wait_out(eng, at, i):
            engine, count = at.emptied(i)
            eng.wait_ge(bank_emptied[engine], count)

        def wait_apart(eng):
            eng.sem_inc(waits_passed, 1)

        def parts_of(task, part):
            if task == "fold":
                w = {FOLD_GCN: mv_w[:, :, :, 1], FOLD_Q: q1_w, FOLD_K: k1_w}[part]
                return w[:, 0].bitcast(F32), w[:, 1], None
            if task in ("h0_turn", "h1_turn"):
                return h_high[:, part, :].bitcast(F32), h_low[:, part, :], None
            dst, bias = {"q0": (q_parts, None), "k0": (k_parts, None), "n_turn": (n_parts, None),
                         "q1": (q_parts, q_b_col), "k1": (k_parts, k_b_col)}[task]
            return (dst[:, part, 0, :], dst[:, part, 1, :].bitcast(F32R),
                    None if bias is None else bias[:, part:part + 1])

        def split_of(i):
            raw, w = ((wq_raw, q0_w), (wk_raw, k0_w), (map_raw, mv_w[:, :, :, 0]))[i]
            return raw, (w[:, 0], w[:, 1])

        block = ctx.enter_context(nc.Block())

        @block.sync
        def _(sp):
            x_tiles = x.rearrange("b (t p) d -> b p t d", p=P)
            out_tiles = out.rearrange("b (t p) d -> b p t d", p=P)
            adj_tiles = adj.rearrange("b (t p) k -> b p t k", p=P)

            def of(tiles, g):
                return tiles[bass.ds(g, 1)].rearrange("a p t d -> (a p) t d")

            def stack_layer0(at):
                wait_out(sp, at, at.latest(N_SLOTS, "q0", 1))
                wait_apart(sp)
                if at.first >= 1:
                    sp.wait_ge(cos_ready, at.graph(-1, Y_SLOTS, Y_SLOTS // 2))
                elif at.first == 0:
                    sp.wait_ge(normed, X_SLOTS)
                for j in range(HC0):
                    for g in range(2):
                        sp.dma_start(q0_stack[D0 * g:D0 * g + D0, j:H0:HC0, :].bitcast(F32),
                                     q_parts[D0 * j:D0 * j + D0, :, g, :]).then_inc(q0_stacked, DMA)
                wait_out(sp, at, at.latest(N_SLOTS, "k0", 1))
                for j in range(HC0):
                    for g in range(2):
                        for which, dst in enumerate((k0_high, k0_low)):
                            sp.dma_start(dst[D0 * g:D0 * g + D0, j:H0:HC0, :].bitcast(F32),
                                         k_parts[D0 * j:D0 * j + D0, :, which, :]).then_inc(k0_stacked, DMA)

            def stack_layer1(at, j):
                if at.first + 1 < graphs:
                    sp.wait_ge(scores_ready, at.units(at.body.unit_number(Y_SLOTS) + QT * (j + 1)))
                    wait_apart(sp)
                if at.first >= 1:
                    sp.wait_ge(cos_ready, at.graph(-1, Y_SLOTS, 3 * GROUP + 2 * j + 2))
                for dst, src, rows in ((stationary_stacks, parts[:, 0:2], (0, 0, 1, 1)),
                                       (moving_stacks, parts[:, 1:3], (0, 1, 0, 1))):
                    for g, which in enumerate(rows):
                        sp.dma_start(dst[D1 * g:D1 * g + D1, :, j:H1:HC1, :].bitcast(F32),
                                     src[D1 * j:D1 * j + D1, :, :, which, :]).then_inc(stacked[j], DMA)

            def load_adj(at, ahead, layer):
                if at.first >= 0:
                    sp.wait_ge(masks_made, mask_number(at, layer) - 1)
                wait_apart(sp)
                sp.dma_start(adj_raw[:, :, :], of(adj_tiles, at.k + ahead)).then_inc(adj_loaded, DMA)

            sp.dma_start(tok[:, :, :], of(x_tiles, 0)).then_inc(tok_loaded, DMA)
            def load(dst, src, loaded):
                sp.dma_start(dst, src.rearrange("(c p) n -> p c n", p=P)).then_inc(loaded, DMA)

            load(wq_raw, wq, wq_loaded)
            load(wk_raw, wk, wk_loaded)
            load(wv_sb[:, :, :], wv, wv_loaded)
            for dst, src in ((map_raw, map_w), (gcn_raw, gcn_w), (map_rows_raw, map_rows), (qw_raw, q_w), (kw_raw, k_w),
                             (wo_sb[:, :, :], wo)):
                load(dst, src, later_loaded)
            for dst, src in ((qk_b_raw[:, 0:DC], qk_b[:, 0:DC]), (qk_b_raw[:, DC:2 * DC], qk_b[:, DC:2 * DC]),
                             (gcn_b_col[:, :], gcn_b), (map_b_col[:, :], map_b_cols)):
                sp.dma_start(dst, src).then_inc(later_loaded, DMA)
            sp.wait_ge(blocks_zeroed, 1)
            for g in range(HC1):
                sp.dma_start(head_blocks[D1 * g:D1 * g + D1, D1 * g:D1 * g + D1], gcn_head_w).then_inc(later_loaded, DMA)
            for dst, src in ((bo_row[:, :], bo), (mv_bias[:, 0], map_b)):
                sp.dma_start(dst, src.partition_broadcast(P)).then_inc(later_loaded, DMA)
            sp.dma_start(x_now[:, :, :], of(x_tiles, 0)).then_inc(x_loaded, DMA)

            def emit(at):
                first, k = at.first, at.k
                has_next, has_this = first + 1 < graphs, 0 <= first < graphs
                if has_next:
                    load_adj(at, 1, 0)
                if first < 0:
                    wait_out(sp, at, at.latest(0, "h0_turn", 1))
                    sp.dma_start(tok[:, :, :], of(x_tiles, k + 2)).then_inc(tok_loaded, DMA)
                if has_next:
                    stack_layer0(at)
                if has_this:
                    load_adj(at, 0, 1)
                    wait_out(sp, at, at.latest(N_SLOTS, "n_turn", 1))
                    if first + 2 < graphs:
                        wait_apart(sp)
                        sp.dma_start(tok[:, :, :], of(x_tiles, k + 2)).then_inc(tok_loaded, DMA)
                    stack_layer1(at, 0)
                if first >= 1:
                    wait_out(sp, at, at.latest(N_SLOTS, "finish", 1))
                    wait_apart(sp)
                    sp.dma_start(of(out_tiles, k - 1), x1_kept[:, :, :]).then_inc(y_stored, DMA)
                if has_this:
                    stack_layer1(at, 1)
                    stack_layer1(at, 2)
                    if has_next:
                        sp.wait_ge(x1_copied, at.graph(0, 1, 1))
                        wait_apart(sp)
                        sp.dma_start(x_now[:, :, :], of(x_tiles, k + 1)).then_inc(x_loaded, DMA)
                    stack_layer1(at, 3)

            walk(sp, emit)
            sp.wait_ge(y_stored, DMA * graphs)

        @block.tensor
        def _(pe):
            def turn(dst, src):
                return nc.tensor.transpose(dst, src, ident[:, :])

            def take_bank(at, n):
                if n >= WORK_BANKS or at.body.before is not None:
                    wait_out(pe, at, n - WORK_BANKS)
                return work_bank[at.bank_ring(n)]

            def product_in_parts(dst, stationary, moving, first, last):
                for n, (a, b) in enumerate(((0, 0), (0, 1), (1, 0))):
                    made = nc.tensor.matmul(dst, stationary[a], moving[b], start=first and n == 0, stop=last and n == 2)
                return made

            def project_features(dst, w, c, i):
                return product_in_parts(dst[:, :], [w[:, a, i, c * P:(c + 1) * P] for a in range(2)],
                                        [h_high[:, i, :], h_low[:, i, :]], i == 0, i == DC - 1)

            def project_tokens(dst, src, w, part, t):
                tile = (2 * part + t) * P
                for i in range(DC):
                    last = nc.tensor.matmul(dst[:, t * dim:(t + 1) * dim], src[:, i, tile:tile + P], w[:, i, :],
                                            start=i == 0, stop=i == DC - 1)
                return last

            def turn_tokens(dst, c):
                for t in range(QT):
                    last = turn(dst[:, t * P:(t + 1) * P], tok[:, t, c * P:(c + 1) * P])
                return last

            def await_operands(at, s, task, ahead, part):
                if task == "fold":
                    pe.wait_ge(later_loaded, LATER_DMAS)
                    if part == FOLD_GCN_B:
                        pe.wait_ge(bias_widened, 1)
                elif task in ("h0_turn", "h1_turn"):
                    pe.wait_ge(normalised[int(task[1])], at.graph(ahead, 1, 1))
                elif task in ("v0", "q0", "k0"):
                    wait_out(pe, at, at.latest(s, "h0_turn", 1))
                    if at.first < 0 and part == 0:
                        if task == "v0":
                            pe.wait_ge(wv_loaded, DMA)
                        else:
                            pe.wait_ge(split_low, 1 if task == "q0" else 2)
                elif task == "out_proj":
                    wait_out(pe, at, at.latest(s, "pv", 1, "X"))
                elif task in ("mv", "q1", "k1"):
                    wait_out(pe, at, at.latest(s, "h1_turn", 1))
                    if at.first == 0 and task == "mv" and part == 0:
                        pe.wait_ge(split_low, 3)
                        wait_out(pe, at, at.latest(s, "fold", FOLD_QK_B))
                elif task == "n_turn":
                    pe.wait_ge(n_ready, at.graph(ahead, 2, 2))
                elif task == "finish":
                    wait_out(pe, at, at.latest(s, "pv", 3, "Y"))

            def fill(at, n, s, piece, is_last):
                task, ahead, part = at.body.bank_tasks[n][1]
                if piece == 0:
                    dst = take_bank(at, n)
                    if task != "pv":
                        await_operands(at, s, task, ahead, part)
                dst = work_bank[at.bank_ring(n)]
                if task == "fold":
                    if part == FOLD_GCN:
                        for i in range(DC):
                            for c in range(DC):
                                col = i * dim + c * P
                                last = nc.tensor.matmul(dst[:, col:col + P], gcn_raw[:, c, i * P:(i + 1) * P],
                                                        head_blocks, start=True, stop=True)
                    elif part == FOLD_GCN_B:
                        for c in range(DC):
                            last = nc.tensor.matmul(dst[:, c * P:(c + 1) * P], gcn_b_wide[:, c, :], head_blocks,
                                                    start=True, stop=True)
                    elif part in (FOLD_Q, FOLD_K):
                        w = qw_raw if part == FOLD_Q else kw_raw
                        for i in range(DC):
                            for c in range(DC):
                                last = nc.tensor.matmul(dst[:, i * dim:(i + 1) * dim], map_rows_raw[:, c, i * P:(i + 1) * P],
                                                        w[:, c, :], start=c == 0, stop=c == DC - 1)
                    else:
                        for col in range(2 * DC):
                            w = (qw_raw, kw_raw)[col // DC]
                            for c in range(DC):
                                out_c = (col % DC) * P
                                last = nc.tensor.matmul(dst[:, col:col + 1], w[:, c, out_c:out_c + P],
                                                        map_b_col[:, c:c + 1], start=c == 0, stop=c == DC - 1)
                elif task in ("h0_turn", "h1_turn", "n_turn"):
                    last = turn_tokens(dst, part)
                elif task == "v0":
                    last = project_tokens(dst, h_whole, wv_sb, part, piece)
                elif task == "out_proj":
                    last = project_tokens(dst, o_t, wo_sb, part, piece)
                elif task in ("q0", "k0", "q1", "k1"):
                    w = {"q0": q0_w, "k0": k0_w, "q1": q1_w, "k1": k1_w}[task]
                    last = project_features(dst, w, part, piece)
                elif task == "mv":
                    tile = slice(part * P, (part + 1) * P)
                    last = product_in_parts(dst[:, :], [h_high[:, piece, tile], h_low[:, piece, tile]],
                                            [mv_w[:, b, piece].rearrange("p w n -> p (w n)") for b in range(2)],
                                            piece == 0, piece == DC - 1)
                elif task == "finish":
                    for t in range(2):
                        tile = (2 * part + t) * P
                        for c in range(DC):
                            col = t * dim + c * P
                            last = turn(dst[:, col:col + P], o_t[:, c, tile:tile + P])
                else:
                    last = times_values(at, s, dst, ahead, part, piece)
                if is_last:
                    last.then_inc(bank_filled, 1)

            def times_values(at, s, dst, kind, group, piece):
                n = at.body.lagged_number(s, LAG_PV)
                if piece == 0:
                    pe.wait_ge(turn_copied, at.units(n + 1))
                    if group == 0:
                        ahead = graph_ahead(s, LAG_PV, kind)
                        pe.wait_ge(v0_kept if kind == "X" else v1_kept, at.graph(ahead, 1, 1))
                for c in range(piece * QT // 2, (piece + 1) * QT // 2):
                    if kind == "X":
                        for h in range(2):
                            col = (2 * group + h) * D0
                            r = at.unit_ring(n + 1 - GROUP + QT * h, TURN_RING)
                            last = nc.tensor.matmul(dst[D0 * h:D0 * h + D0, :], v0[:, c, col:col + D0],
                                                    prob_t[:, r:r + QT, c, :], start=c == 0, stop=c == QT - 1,
                                                    skip_group_check=True)
                    else:
                        for j in range(HC1):
                            col = ((group // 2) * HC1 + j) * D1
                            r = at.unit_ring(n + 1 - GROUP + 2 * j, TURN_RING)
                            last = nc.tensor.matmul(dst[D1 * j:D1 * j + D1, 0:HALF], v1[:, c, col:col + D1],
                                                    prob_t[:, r:r + 2, c, :], start=c == 0, stop=c == QT - 1,
                                                    skip_group_check=True)
                return last

            def scores(at, s, kind, u):
                n = at.body.unit_number(s)
                if at.n_units + n >= 2:
                    pe.wait_ge(masked, at.units(n - 1))
                dst = score_bank[at.unit_ring(n, 2)]
                if kind == "X":
                    head, _, t = unit_x(u)
                    if u == 0:
                        pe.wait_ge(q0_stacked, at.graph(1, Q0_DMAS, Q0_DMAS))
                        pe.wait_ge(k0_stacked, at.graph(1, K0_DMAS, K0_DMAS))
                    q = q0_stack[:, head, t * P:(t + 1) * P]
                    nc.tensor.matmul(dst[:, :], q, k0_high[:, head, :], start=True, stop=False)
                    nc.tensor.matmul(dst[:, :], q, k0_low[:, head, :], start=False, stop=True).then_inc(scores_ready, 1)
                else:
                    head, j, t, _ = unit_y(u)
                    if u < GROUP and u % 2 == 0:
                        pe.wait_ge(stacked[j], at.graph(-1, STACK1_DMAS, STACK1_DMAS))
                    nc.tensor.matmul(dst[:, :], q1_stack[:, head, t * P:(t + 1) * P], k1_stack[:, head, :],
                                     start=True, stop=True).then_inc(scores_ready, 1)

            def cosines(at, s, u):
                head, _, t, _ = unit_y(u)
                if u >= 1:
                    pe.wait_ge(picked, at.graph(graph_ahead(s, LAG_COS, "Y"), Y_SLOTS, u))
                nc.tensor.matmul(cos_bank[:, :], ns_stack[:, head, t * P:(t + 1) * P], nm_stack[:, head, :],
                                 start=True, stop=True).then_inc(cos_ready, 1)

            def turn_weights(at, s, kind, u):
                n = at.body.lagged_number(s, LAG_TURN)
                ahead = graph_ahead(s, LAG_TURN, kind)
                if kind == "X":
                    pe.wait_ge(normed, at.graph(ahead, X_SLOTS, u + 1))
                else:
                    pe.wait_ge(picked, at.graph(ahead, Y_SLOTS, u + 1))
                if at.n_units + n >= 2:
                    pe.wait_ge(turn_copied, at.units(n - 1))
                dst, r = turn_bank[at.unit_ring(n, 2)], at.unit_ring(n, PROB_RING)
                for c in range(QT):
                    last = turn(dst[:, c * P:(c + 1) * P], prob[:, r, c * P:(c + 1) * P])
                last.then_inc(turned, 1)

            pe.wait_ge(consts_made, 1)

            def emit(at):
                for s in range(N_SLOTS):
                    if at.body.units[s]:
                        scores(at, s, *at.body.units[s])
                    if at.body.lagged(s, LAG_TURN):
                        turn_weights(at, s, *at.body.lagged(s, LAG_TURN))
                    for n, start, piece, is_last in at.body.pieces[s]:
                        fill(at, n, start, piece, is_last)
                    done = at.body.lagged(s, LAG_COS)
                    if done and done[0] == "Y":
                        cosines(at, s, done[1])

            walk(pe, emit)

        @block.vector
        def _(dve):
            emptied = bank_emptied["dve"]

            def mask_and_max(at, s, kind, u):
                n = at.body.unit_number(s)
                dve.wait_ge(scores_ready, at.units(n + 1))
                if at.n_units + n >= PROB_RING:
                    dve.wait_ge(turned, at.units(n + 1 - PROB_RING))
                if kind == "X":
                    t, mask, scale = unit_x(u)[2], mask0, C0
                    if u == 0:
                        dve.wait_ge(masks_made, mask_number(at, 0))
                else:
                    t, mask, scale = unit_y(u)[2], mask1, C1
                    if u == 0:
                        dve.wait_ge(masks_made, at.graph(0, 2, 1 if at.first < graphs else 0))
                wait_apart(dve)
                r = at.unit_ring(n, PROB_RING)
                nc.vector.tensor_tensor_reduce(out=prob[:, r, :], in0=score_bank[at.unit_ring(n, 2)][:, :],
                                               in1=mask[:, t, :], scale=-scale, scalar=BIG, op0=ALU.add, op1=ALU.min,
                                               accum_out=row_min[:, r:r + 1]).then_inc(masked, 1)

            def select(at, s, kind, u):
                n = at.body.lagged_number(s, LAG_SELECT)
                dve.wait_ge(exped, at.units(n + 1))
                r = at.unit_ring(n, PROB_RING)
                if kind == "X":
                    nc.vector.reciprocal(inv0[:, u:u + 1], sum0[:, u:u + 1]).then_inc(inverted, 1)
                else:
                    head, _, t, _ = unit_y(u)
                    dve.wait_ge(cos_ready, at.graph(graph_ahead(s, LAG_SELECT, kind), Y_SLOTS, u + 1))
                    nc.vector.scalar_tensor_tensor(out=prob[:, r, :], in0=cos_bank[:, :], scalar=COS_MIN,
                                                   in1=prob[:, r, :], op0=ALU.is_gt, op1=ALU.mult,
                                                   accum_out=picked1[:, t, head:head + 1]).then_inc(picked, 1)

            def row_stats(at, ahead, layer, src, part):
                for t in (2 * part, 2 * part + 1):
                    last = nc.vector.bn_stats(stats[:, t, :], src[:, t, :])
                if part == 0:
                    return
                last.then_inc(stats_taken[layer], 1)
                dve.wait_ge(stats_taken[layer], at.graph(ahead, 1, 1))
                if at.first + ahead >= 1:
                    dve.wait_ge(normalised[layer], at.graph(ahead, 1, 0))
                wait_apart(dve)
                for t in range(QT):
                    last = nc.vector.bn_aggr(mean_var[layer][:, t, :], stats[:, t, :])
                last.then_inc(stats_ready[layer], 1)

            def row_factors(at, ahead):
                dve.wait_ge(picked, at.graph(ahead, Y_SLOTS, Y_SLOTS))
                nc.vector.tensor_tensor(factor[:, :, :], sum1[:, :, :], picked1[:, :, :], ALU.add).then_inc(factor_step, 1)
                nc.vector.tensor_scalar(keep_row[:, :], mask1[:, :, 0], NEG1 / 2, None, ALU.is_gt).then_inc(factor_step, 1)
                dve.wait_ge(factor_step, at.graph(ahead, 3, 2))
                nc.vector.reciprocal(factor[:, :, :], factor[:, :, :]).then_inc(factor_step, 1)
                dve.wait_ge(factor_step, at.graph(ahead, 3, 3))
                nc.vector.tensor_tensor(factor[:, :, :], factor[:, :, :],
                                        keep_row[:, :].unsqueeze(2).broadcast_to([P, QT, H1]),
                                        ALU.mult).then_inc(factors_ready, 1)

            def empty(at, n, s, task, ahead, part):
                dve.wait_ge(bank_filled, at.banks(n + 1))
                src = work_bank[at.bank_ring(n)]
                src_tiles = src[:, :].rearrange("p (t d) -> p t d", t=2)
                pair = slice(2 * part, 2 * part + 2)
                if task == "fold" and part == FOLD_GCN_B:
                    nc.vector.tensor_copy(mv_bias[:, 1], src[:, 0:dim]).then_inc(emptied, 1)
                elif task == "fold" and part == FOLD_QK_B:
                    nc.vector.tensor_tensor(qk_b_cols[:, :], src[:, 0:2 * DC], qk_b_raw[:, :], ALU.add).then_inc(emptied, 1)
                elif task == "out_proj":
                    dve.wait_ge(bo_added, at.graph(ahead, 1, 1))
                    nc.vector.tensor_tensor(x_now[:, pair, :], src_tiles, x_now[:, pair, :], ALU.add).then_inc(emptied, 1)
                elif task == "mv":
                    if part == 0:
                        if at.first + 1 < graphs:
                            dve.wait_ge(v0_kept, at.graph(1, 1, 1))
                        else:
                            dve.wait_ge(v1_kept, at.graph(-1, 1, 1))
                        if at.first == 0:
                            wait_out(dve, at, at.latest(s, "fold", FOLD_QK_B))
                    nc.vector.tensor_tensor(tok_v[:, :, part, :], src_tiles, mv_bias[:, :, :], ALU.add).then_inc(emptied, 1)
                elif task == "finish":
                    dve.wait_ge(factors_ready, at.graph(ahead, 1, 1))
                    heads = factor[:, pair, :].rearrange("p t h -> p (t h)").unsqueeze(2).broadcast_to([P, 2 * H1, D1])
                    src_heads = src[:, :].rearrange("p (h d) -> p h d", d=D1)
                    nc.vector.tensor_tensor(src_heads, src_heads, heads, ALU.mult).then_inc(scaled, 1)
                    dve.wait_ge(scaled, at.graph(ahead, 2, part + 1))
                    dve.wait_ge(x1_copied, at.graph(ahead, 1, 1))
                    nc.vector.scalar_tensor_tensor(out=x1_kept[:, pair, :], in0=src_tiles, scalar=0.0,
                                                   in1=x1_kept[:, pair, :], op0=ALU.max, op1=ALU.add).then_inc(emptied, 1)
                else:
                    high, low, bias = parts_of(task, part)
                    count = {FOLD_GCN: 1, FOLD_Q: 2, FOLD_K: 3}[part] if task == "fold" else at.graph(ahead, DC, part + 1)
                    dve.wait_ge(high_ready[task], count)
                    whole = src_tiles if task == "fold" else src[:, :]
                    if task == "h0_turn":
                        nc.vector.tensor_scalar(h_whole[:, part, :], whole, 0.0, None, ALU.max)
                    if task in ("h0_turn", "h1_turn"):
                        nc.vector.scalar_tensor_tensor(out=low, in0=whole, scalar=0.0, in1=high, op0=ALU.max,
                                                       op1=ALU.subtract).then_inc(emptied, 1)
                    elif bias is None:
                        nc.vector.tensor_tensor(low, whole, high, ALU.subtract).then_inc(emptied, 1)
                    else:
                        nc.vector.scalar_tensor_tensor(out=low, in0=whole, scalar=bias, in1=high,
                                                       op0=ALU.add, op1=ALU.subtract).then_inc(emptied, 1)

            def step(at, s, task, ahead, part):
                if task == "ln0_stats":
                    dve.wait_ge(tok_loaded, at.graph(ahead, DMA, DMA))
                    row_stats(at, ahead, 0, tok, part)
                elif task == "ln1_stats":
                    wait_out(dve, at, at.latest(s, "out_proj", part))
                    row_stats(at, ahead, 1, x_now, part)
                elif task == "m_sums":
                    dve.wait_ge(squared, at.graph(ahead, QT, 2 * part + 2))
                    if at.first + ahead >= 1 and part == 0:
                        dve.wait_ge(inv_norm_ready, at.graph(ahead, 2, 0))
                    nc.vector.reduce_sum(norm2[:, part * 2 * H1:(part + 1) * 2 * H1],
                                         squares[:, part * 2 * dim:(part + 1) * 2 * dim].rearrange(
                                             "p (a d) -> p a d", d=D1), AX_X).then_inc(summed, 1)
                elif task == "split":
                    raw, dst = split_of(part)
                    dve.wait_ge(split_high, part + 1)
                    nc.vector.tensor_tensor(dst[1], raw, dst[0].bitcast(F32), ALU.subtract).then_inc(split_low, 1)
                    if part == 2:
                        dve.wait_ge(later_loaded, LATER_DMAS)
                        nc.vector.tensor_copy(gcn_b_wide, gcn_b_col[:, :].unsqueeze(2).broadcast_to(
                            [P, DC, P])).then_inc(bias_widened, 1)
                elif task == "row_factors":
                    row_factors(at, ahead)
                elif task == "keep_v1":
                    if part == 0:
                        if at.first >= 1:
                            dve.wait_ge(bank_filled, at.banks(at.latest(s, "pv", 3, "Y") + 1))
                        wait_out(dve, at, at.latest(s, "mv", QT - 1))
                    copied = nc.vector.tensor_copy(v1[:, 2 * part:2 * part + 2, :], v_next[:, 2 * part:2 * part + 2, :])
                    if part == 1:
                        copied.then_inc(v1_kept, 1)
                elif task == "keep_x1":
                    if at.first >= 1:
                        dve.wait_ge(y_stored, at.graph(-1, DMA, DMA))
                    nc.vector.tensor_copy(x1_kept[:, :, :], x_now[:, :, :]).then_inc(x1_copied, 1)

            def emit(at):
                for s in range(N_SLOTS):
                    if at.body.units[s]:
                        mask_and_max(at, s, *at.body.units[s])
                    for n in at.body.emptying[s]:
                        task, ahead, part = at.body.bank_tasks[n][1]
                        if PSUM_TASKS[task] == "dve":
                            empty(at, n, s, task, ahead, part)
                    if at.body.lagged(s, LAG_SELECT):
                        select(at, s, *at.body.lagged(s, LAG_SELECT))
                    for task, ahead, part in at.body.tasks[s]:
                        if task not in PSUM_TASKS:
                            step(at, s, task, ahead, part)

            walk(dve, emit)

        @block.scalar
        def _(act):
            emptied = bank_emptied["act"]

            def exp(at, s, kind, u):
                n = at.body.unit_number(s)
                act.wait_ge(masked, at.units(n + 1))
                r = at.unit_ring(n, PROB_RING)
                if kind == "X":
                    total = sum0[:, u:u + 1]
                else:
                    head, _, t, _ = unit_y(u)
                    total = sum1[:, t, head:head + 1]
                nc.scalar.activation(prob[:, r, :], prob[:, r, :], ACT.Exp, bias=row_min[:, r:r + 1], scale=-1.0,
                                     accum_out=total).then_inc(exped, 1)

            def copy_turned(at, s, kind, u):
                n = at.body.lagged_number(s, LAG_TURN)
                act.wait_ge(turned, at.units(n + 1))
                if u % GROUP == TURN_RING - GROUP and at.n_units + n >= GROUP:
                    act.wait_ge(bank_filled, at.banks(at.latest(s, "pv") + 1))
                nc.scalar.copy(prob_t[:, at.unit_ring(n, TURN_RING)].rearrange("p c q -> p (c q)"),
                               turn_bank[at.unit_ring(n, 2)][:, :]).then_inc(turn_copied, 1)

            def empty(at, n, s, task, ahead, part):
                if task in ("out_proj", "mv", "finish") or task == "fold" and part in (FOLD_GCN_B, FOLD_QK_B):
                    return
                act.wait_ge(bank_filled, at.banks(n + 1))
                src = work_bank[at.bank_ring(n)]
                if task == "pv":
                    if ahead == "X":
                        nc.scalar.copy(o_t[:, part, :], src[:, :]).then_inc(emptied, 1)
                    else:
                        half = (part % 2) * HALF
                        nc.scalar.copy(o_t[:, part // 2, half:half + HALF], src[:, 0:HALF]).then_inc(emptied, 1)
                elif task == "v0":
                    if at.first >= 1 and part == 0:
                        act.wait_ge(v1_kept, at.graph(0, 1, 0))
                    nc.scalar.copy(v_next[:, 2 * part:2 * part + 2, :],
                                   src[:, :].rearrange("p (t d) -> p t d", t=2)).then_inc(emptied, 1)
                else:
                    if part == 0 and task in ("q0", "k0", "n_turn") and at.first >= 1:
                        for j in range(HC1):
                            act.wait_ge(stacked[j], at.graph(0, STACK1_DMAS, 0))
                    if part == 0 and task in ("q1", "k1"):
                        latest = 1 if at.first + 1 < graphs else 0
                        if task == "q1":
                            act.wait_ge(q0_stacked, at.graph(latest, Q0_DMAS, Q0_DMAS))
                        else:
                            act.wait_ge(k0_stacked, at.graph(latest, K0_DMAS, K0_DMAS))
                    high, _, bias = parts_of(task, part)
                    high = high.bitcast(F32R)
                    whole = src[:, :].rearrange("p (t d) -> p t d", t=2) if task == "fold" else src[:, :]
                    if task in ("h0_turn", "h1_turn"):
                        nc.scalar.activation(high, whole, ACT.Relu).then_inc(high_ready[task], 1)
                    elif bias is None:
                        nc.scalar.activation(high, whole, ACT.Identity).then_inc(high_ready[task], 1)
                    else:
                        nc.scalar.activation(high, whole, ACT.Identity, bias=bias).then_inc(high_ready[task], 1)

            def emit(at):
                for s in range(N_SLOTS):
                    for n in at.body.emptying[s]:
                        empty(at, n, s, *at.body.bank_tasks[n][1])
                    if at.body.lagged(s, LAG_TURN):
                        copy_turned(at, s, *at.body.lagged(s, LAG_TURN))
                    if at.body.units[s]:
                        exp(at, s, *at.body.units[s])
                    for task, ahead, part in at.body.tasks[s]:
                        if task == "m_square":
                            if part == 0 and at.first >= 1:
                                for j in range(HC1):
                                    act.wait_ge(stacked[j], at.graph(0, STACK1_DMAS, 0))
                            wait_out(act, at, at.latest(s, "mv", part))
                            nc.scalar.activation(squares[:, part * dim:(part + 1) * dim], tok[:, part, :],
                                                 ACT.Square).then_inc(squared, 1)
                        elif task == "split":
                            raw, dst = split_of(part)
                            act.wait_ge((wq_loaded, wk_loaded, later_loaded)[part], (DMA, DMA, LATER_DMAS)[part])
                            nc.scalar.activation(dst[0], raw, ACT.Identity).then_inc(split_high, 1)

            walk(act, emit)

        @block.gpsimd
        def _(pool):
            def normalise(at, ahead, layer, src, t):
                if t == 0:
                    pool.wait_ge(stats_ready[layer], at.graph(ahead, 1, 1))
                    wait_apart(pool)
                    nc.gpsimd.tensor_scalar(minus_mean[:, :], mean_var[layer][:, :, 0], -1.0, 0.0,
                                            ALU.mult, ALU.add).then_inc(norm_step[layer], 1)
                    nc.gpsimd.tensor_scalar(var_eps[:, :], mean_var[layer][:, :, 1], LN_EPS, 1.0,
                                            ALU.add, ALU.mult).then_inc(norm_step[layer], 1)
                    pool.wait_ge(norm_step[layer], at.graph(ahead, 3, 2))
                    nc.gpsimd.tensor_tensor(rstd[:, :], var_eps[:, :], minus_half[:, 0:QT], ALU.pow).then_inc(norm_step[layer], 1)
                    pool.wait_ge(norm_step[layer], at.graph(ahead, 3, 3))
                    wait_apart(pool)
                done = nc.gpsimd.tensor_scalar(tok[:, t, :], src[:, t, :], minus_mean[:, t:t + 1], rstd[:, t:t + 1],
                                               ALU.add, ALU.mult)
                if t == QT - 1:
                    done.then_inc(normalised[layer], 1)

            def make_mask(at, layer, t):
                number = mask_number(at, layer)
                if layer == 0:
                    pool.wait_ge(adj_loaded, number * DMA)
                    if at.body.before is not None:
                        pool.wait_ge(masked, at.units(0))
                    wait_apart(pool)
                    nc.gpsimd.tensor_scalar(mask0[:, :, :], adj_raw[:, :, :], -1.0, -NEG0,
                                            ALU.add, ALU.mult).then_inc(masks_made, 1)
                    return
                if t == 0:
                    pool.wait_ge(adj_loaded, number * DMA)
                    if at.first >= 1:
                        pool.wait_ge(factors_ready, at.graph(0, 1, 0))
                    wait_apart(pool)
                done = nc.gpsimd.tensor_scalar(mask1[:, t, :], adj_raw[:, t, :], NEG1, 0.0, ALU.mult, ALU.add)
                if t == QT - 1:
                    done.then_inc(masks_made, 1)

            def step(at, s, task, ahead, part):
                if task == "ln0_apply":
                    normalise(at, ahead, 0, tok, part)
                elif task == "ln1_apply":
                    if part == 0:
                        wait_out(pool, at, at.latest(s, "h0_turn" if at.first + 1 < graphs else "n_turn", 1))
                    normalise(at, ahead, 1, x_now, part)
                elif task == "add_bo":
                    pool.wait_ge(x_loaded, at.graph(ahead, DMA, DMA))
                    if at.first == 0:
                        pool.wait_ge(later_loaded, LATER_DMAS)
                    nc.gpsimd.tensor_tensor(x_now[:, :, :], x_now[:, :, :],
                                            bo_row[:, :].unsqueeze(1).broadcast_to([P, QT, dim]),
                                            ALU.add).then_inc(bo_added, 1)
                elif task in ("mask0", "mask1"):
                    make_mask(at, int(task[-1]), part)
                elif task == "m_norms":
                    half = slice(part * 2 * H1, (part + 1) * 2 * H1)
                    pool.wait_ge(summed, at.graph(ahead, 2, part + 1))
                    wait_apart(pool)
                    nc.gpsimd.tensor_scalar(floored[:, half], norm2[:, half], NORM_FLOOR, BIG,
                                            ALU.max, ALU.min).then_inc(norms_floored, 1)
                    pool.wait_ge(norms_floored, at.graph(ahead, 2, part + 1))
                    nc.gpsimd.tensor_tensor(inv_norm[:, half], floored[:, half], minus_half[:, half],
                                            ALU.pow).then_inc(inv_norm_ready, 1)
                elif task == "n_scale":
                    pool.wait_ge(inv_norm_ready, at.graph(ahead, 2, part + 1))
                    half = slice(part * 2 * H1, (part + 1) * 2 * H1)
                    heads = tok[:, :, :].rearrange("p t d -> p (t d)").rearrange("p (a d) -> p a d", d=D1)[:, half]
                    nc.gpsimd.tensor_tensor(heads, heads, inv_norm[:, half].unsqueeze(2).broadcast_to([P, 2 * H1, D1]),
                                            ALU.mult).then_inc(n_ready, 1)
                elif task == "keep_v0":
                    if at.first >= 0:
                        pool.wait_ge(bank_filled, at.banks(at.latest(s, "pv", 1, "X") + 1))
                    wait_out(pool, at, at.latest(s, "v0", 1))
                    wait_apart(pool)
                    nc.gpsimd.tensor_scalar(v0[:, :, :], v_next, 1.0, 1.0, ALU.mult, ALU.mult).then_inc(v0_kept, 1)
            nc.gpsimd.memset(head_blocks, 0.0).then_inc(blocks_zeroed, 1)
            nc.gpsimd.memset(minus_half[:, :], -0.5)
            nc.gpsimd.memset(ident[:, :], 0.0).then_inc(ident_zeroed, 1)
            pool.wait_ge(ident_zeroed, 1)
            nc.gpsimd.affine_select(out=ident[:, :], in_=ident[:, :], compare_op=ALU.not_equal, fill=1.0, base=0,
                                    pattern=[[-1, P]], channel_multiplier=1).then_inc(consts_made, 1)
            pool.wait_ge(consts_made, 1)

            def emit(at):
                for s in range(N_SLOTS):
                    done = at.body.lagged(s, LAG_SELECT)
                    if done and done[0] == "X":
                        u, r = done[1], at.unit_ring(at.body.lagged_number(s, LAG_SELECT), PROB_RING)
                        pool.wait_ge(inverted, at.graph(graph_ahead(s, LAG_SELECT, "X"), X_SLOTS, u + 1))
                        wait_apart(pool)
                        nc.gpsimd.tensor_scalar(prob[:, r, :], prob[:, r, :], inv0[:, u:u + 1], 1.0,
                                                ALU.mult, ALU.mult).then_inc(normed, 1)
                    for task, ahead, part in at.body.tasks[s]:
                        if task not in PSUM_TASKS:
                            step(at, s, task, ahead, part)

            walk(pool, emit)


_OUT_SHAPE = (16, 512, 256)


def kernel(**inputs):
    import numpy as np
    import concourse.bacc as bacc
    from concourse.bass_utils import run_bass_kernel_spmd

    def laid(name, turned=False):
        a = np.asarray(inputs[name])
        return np.ascontiguousarray(a.T if turned else a)

    def column(name):
        return np.ascontiguousarray(np.asarray(inputs[name]).reshape(-1, P).T)

    arrays = {
        "x": laid("x"), "adj": laid("adj"),
        "wq": laid("L0_gnn_Wq"), "wk": laid("L0_gnn_Wk"), "wv": laid("L0_gnn_Wv"), "wo": laid("L0_gnn_Wo"),
        "bo": laid("L0_gnn_bo"),
        "map_w": laid("L1_gnn_map_w", True), "map_rows": laid("L1_gnn_map_w"), "map_b": laid("L1_gnn_map_b"),
        "map_b_cols": column("L1_gnn_map_b"),
        "qk_b": np.concatenate([column("L1_gnn_q_b"), column("L1_gnn_k_b")], axis=1),
        "q_w": laid("L1_gnn_q_w", True), "k_w": laid("L1_gnn_k_w", True),
        "gcn_w": laid("L1_gnn_gcn_map_w"), "gcn_b": column("L1_gnn_gcn_map_b"),
        "gcn_head_w": laid("L1_gnn_gcn_W", True),
    }
    nc = bacc.Bacc("TRN2", target_bir_lowering=False, num_devices=1)
    args = [nc.dram_tensor(f"{n}_dram", a.shape, mybir.dt.from_np(a.dtype), kind="ExternalInput").ap()
            for n, a in arrays.items()]
    out = nc.dram_tensor("out_dram", _OUT_SHAPE, F32, kind="ExternalOutput").ap()
    attention_layers(nc, *args, out)
    r = run_bass_kernel_spmd(nc, [{f"{n}_dram": a for n, a in arrays.items()}], core_ids=[0])
    return r.results[0]["out_dram"]
```
